# Optimizing a Trainium2 kernel written in Bass

```python
import numpy as np
import jax
import jax.numpy as jnp

def _softmax(x, axis=-1):
    return jax.nn.softmax(x, axis=axis)

def _gelu(x):
    return jax.nn.gelu(x, approximate=True)

def _silu(x):
    return jax.nn.silu(x)

def _sigmoid(x):
    return jax.nn.sigmoid(x)

def _layernorm(x, axis=-1, eps=1e-05):
    m = jnp.mean(x, axis=axis, keepdims=True)
    v = jnp.var(x, axis=axis, keepdims=True)
    return (x - m) / jnp.sqrt(v + eps)

def _scatter_add(tgt, idx, src, axis=0):
    return tgt.at[idx].add(src)

def _segment_sum(src, seg, n):
    return jax.ops.segment_sum(src, seg, n)
kernel_name = 'mk_conv_seq_d2_conv_nchw512_r2_c874f6'

def setup_inputs(seed: int=0):
    np.random.seed(seed)
    _w = jnp.asarray

    def _rec_inputs():
        import jax
        import jax.numpy as jnp
        _gk = jax.random.key(seed)
        x = 7.22e-05 + 1 * jax.random.normal(jax.random.fold_in(_gk, 1), (4, 256, 32, 32), jnp.float32)
        return x
    x = _rec_inputs()

    def _L0_conv_setup():
        import jax, jax.numpy as jnp
        import numpy as np
        C = 256
        GROUPS = 32
        EPS = 1e-05

        def group_norm(x, gamma, beta):
            B, Ch, H, W = x.shape
            xg = x.reshape(B, GROUPS, Ch // GROUPS, H, W)
            mu = xg.mean(axis=(2, 3, 4), keepdims=True)
            var = xg.var(axis=(2, 3, 4), keepdims=True)
            xn = ((xg - mu) * jax.lax.rsqrt(var + EPS)).reshape(B, Ch, H, W)
            return xn * gamma[None, :, None, None] + beta[None, :, None, None]

        def conv1x1(x, w, b):
            return jnp.einsum('bchw,oc->bohw', x, w) + b[None, :, None, None]
        key = jax.random.key(seed)
        ks = jax.random.split(key, 12)
        B, H, W = (4, 32, 32)
        s = 1.0 / np.sqrt(C)
        inp = {'x': jax.random.normal(ks[0], (B, C, H, W), dtype=jnp.float32), 'gn_w': jnp.ones((C,), dtype=jnp.float32), 'gn_b': jnp.zeros((C,), dtype=jnp.float32), 'wq': jax.random.uniform(ks[1], (C, C), jnp.float32, -s, s), 'bq': jax.random.uniform(ks[2], (C,), jnp.float32, -s, s), 'wk': jax.random.uniform(ks[3], (C, C), jnp.float32, -s, s), 'bk': jax.random.uniform(ks[4], (C,), jnp.float32, -s, s), 'wv': jax.random.uniform(ks[5], (C, C), jnp.float32, -s, s), 'bv': jax.random.uniform(ks[6], (C,), jnp.float32, -s, s), 'wo': jax.random.uniform(ks[7], (C, C), jnp.float32, -s, s), 'bo': jax.random.uniform(ks[8], (C,), jnp.float32, -s, s)}
        return inp
    _L0_conv_all = _L0_conv_setup()
    _L0_conv_in = {k: v for k, v in _L0_conv_all.items() if k in ('gn_w', 'gn_b', 'wq', 'bq', 'wk', 'bk', 'wv', 'bv', 'wo', 'bo')}
    del _L0_conv_all

    def _L1_conv_setup():
        import jax, jax.numpy as jnp
        import numpy as np

        def conv1x1(x, w, b):
            return jnp.einsum('bchw,oc->bohw', x, w) + b[None, :, None, None]
        key = jax.random.key(seed)
        ks = jax.random.split(key, 8)
        B, C, H, W = (4, 256, 32, 32)
        C8 = C // 8
        s = 1.0 / np.sqrt(C)
        return {'x': jax.random.normal(ks[0], (B, C, H, W), dtype=jnp.float32), 'wb': jax.random.normal(ks[1], (C8, C), dtype=jnp.float32) * s, 'bb': jnp.zeros((C8,), dtype=jnp.float32), 'wc': jax.random.normal(ks[2], (C8, C), dtype=jnp.float32) * s, 'bc': jnp.zeros((C8,), dtype=jnp.float32), 'wd': jax.random.normal(ks[3], (C, C), dtype=jnp.float32) * s, 'bd': jnp.zeros((C,), dtype=jnp.float32), 'alpha': jnp.zeros((1,), dtype=jnp.float32), 'beta': jnp.zeros((1,), dtype=jnp.float32)}
    _L1_conv_all = _L1_conv_setup()
    _L1_conv_in = {k: v for k, v in _L1_conv_all.items() if k in ('wb', 'bb', 'wc', 'bc', 'wd', 'bd', 'alpha', 'beta')}
    del _L1_conv_all
    return {'x': x, 'L0_conv_gn_w': _L0_conv_in['gn_w'], 'L0_conv_gn_b': _L0_conv_in['gn_b'], 'L0_conv_wq': _L0_conv_in['wq'], 'L0_conv_bq': _L0_conv_in['bq'], 'L0_conv_wk': _L0_conv_in['wk'], 'L0_conv_bk': _L0_conv_in['bk'], 'L0_conv_wv': _L0_conv_in['wv'], 'L0_conv_bv': _L0_conv_in['bv'], 'L0_conv_wo': _L0_conv_in['wo'], 'L0_conv_bo': _L0_conv_in['bo'], 'L1_conv_wb': _L1_conv_in['wb'], 'L1_conv_bb': _L1_conv_in['bb'], 'L1_conv_wc': _L1_conv_in['wc'], 'L1_conv_bc': _L1_conv_in['bc'], 'L1_conv_wd': _L1_conv_in['wd'], 'L1_conv_bd': _L1_conv_in['bd'], 'L1_conv_alpha': _L1_conv_in['alpha'], 'L1_conv_beta': _L1_conv_in['beta']}

def reference(x, L0_conv_gn_w, L0_conv_gn_b, L0_conv_wq, L0_conv_bq, L0_conv_wk, L0_conv_bk, L0_conv_wv, L0_conv_bv, L0_conv_wo, L0_conv_bo, L1_conv_wb, L1_conv_bb, L1_conv_wc, L1_conv_bc, L1_conv_wd, L1_conv_bd, L1_conv_alpha, L1_conv_beta):
    import jax
    import jax.numpy as jnp

    def _L0_conv_ref(x, gn_w, gn_b, wq, bq, wk, bk, wv, bv, wo, bo):
        import jax, jax.numpy as jnp
        import numpy as np
        C = 256
        GROUPS = 32
        EPS = 1e-05

        def group_norm(x, gamma, beta):
            B, Ch, H, W = x.shape
            xg = x.reshape(B, GROUPS, Ch // GROUPS, H, W)
            mu = xg.mean(axis=(2, 3, 4), keepdims=True)
            var = xg.var(axis=(2, 3, 4), keepdims=True)
            xn = ((xg - mu) * jax.lax.rsqrt(var + EPS)).reshape(B, Ch, H, W)
            return xn * gamma[None, :, None, None] + beta[None, :, None, None]

        def conv1x1(x, w, b):
            return jnp.einsum('bchw,oc->bohw', x, w) + b[None, :, None, None]
        B, Ch, H, W = x.shape
        h = group_norm(x, gn_w, gn_b)
        q = conv1x1(h, wq, bq).reshape(B, Ch, H * W)
        k = conv1x1(h, wk, bk).reshape(B, Ch, H * W)
        v = conv1x1(h, wv, bv).reshape(B, Ch, H * W)
        scale = 1.0 / jnp.sqrt(jnp.float32(Ch))
        w = jnp.einsum('bcq,bck->bqk', q, k) * scale
        w = jax.nn.softmax(w, axis=-1)
        o = jnp.einsum('bqk,bck->bcq', w, v).reshape(B, Ch, H, W)
        o = conv1x1(o, wo, bo)
        return x + o

    def _L1_conv_ref(x, wb, bb, wc, bc, wd, bd, alpha, beta):
        import jax, jax.numpy as jnp
        import numpy as np

        def conv1x1(x, w, b):
            return jnp.einsum('bchw,oc->bohw', x, w) + b[None, :, None, None]
        B, C, H, W = x.shape
        N = H * W
        fa = x.reshape(B, C, N)
        att = jnp.einsum('bcn,bdn->bcd', fa, fa)
        att_new = jnp.max(att, axis=-1, keepdims=True) - att
        att_c = jax.nn.softmax(att_new, axis=-1)
        feat_e = jnp.einsum('bcd,bdn->bcn', att_c, fa).reshape(B, C, H, W)
        out_ch = beta * feat_e + x
        fb = conv1x1(x, wb, bb).reshape(B, -1, N)
        fc = conv1x1(x, wc, bc).reshape(B, -1, N)
        att_s = jax.nn.softmax(jnp.einsum('bkn,bkm->bnm', fb, fc), axis=-1)
        fd = conv1x1(x, wd, bd).reshape(B, C, N)
        feat_p = jnp.einsum('bcm,bnm->bcn', fd, att_s).reshape(B, C, H, W)
        out_pos = alpha * feat_p + x
        return out_ch + out_pos

    def _gn(v, G=32, eps=1e-05):
        B_, C_, H_, W_ = v.shape
        g = v.reshape(B_, G, C_ // G, H_, W_)
        m = jnp.mean(g, axis=(2, 3, 4), keepdims=True)
        s = jnp.var(g, axis=(2, 3, 4), keepdims=True)
        return ((g - m) / jnp.sqrt(s + eps)).reshape(v.shape)

    def _ln_c(v, eps=1e-06):
        m = jnp.mean(v, axis=1, keepdims=True)
        s = jnp.var(v, axis=1, keepdims=True)
        return (v - m) / jnp.sqrt(s + eps)

    def _ln_t(v, eps=1e-05):
        m = jnp.mean(v, axis=-1, keepdims=True)
        s = jnp.var(v, axis=-1, keepdims=True)
        return (v - m) / jnp.sqrt(s + eps)

    def _to_tokens(v):
        B_, C_, H_, W_ = v.shape
        return v.reshape(B_, C_, H_ * W_).transpose(0, 2, 1)

    def _from_tokens(t, like):
        B_, C_, H_, W_ = like.shape
        return t.transpose(0, 2, 1).reshape(B_, C_, H_, W_)
    x = _L0_conv_ref(x, L0_conv_gn_w, L0_conv_gn_b, L0_conv_wq, L0_conv_bq, L0_conv_wk, L0_conv_bk, L0_conv_wv, L0_conv_bv, L0_conv_wo, L0_conv_bo)
    x = _L1_conv_ref(x, L1_conv_wb, L1_conv_bb, L1_conv_wc, L1_conv_bc, L1_conv_wd, L1_conv_bd, L1_conv_alpha, L1_conv_beta)
    return x

_drawn_inputs = setup_inputs


def setup_inputs(seed=0):
    import zlib

    import numpy as np

    out = dict(_drawn_inputs(seed))
    spreads = {'L0_conv_gn_w': (1.0, 0.6),
     'L0_conv_gn_b': (0.0, 0.1),
     'L1_conv_bb': (0.0, 0.1),
     'L1_conv_bc': (0.0, 0.1),
     'L1_conv_bd': (0.0, 0.1)}
    factors = {'L0_conv_wq': 6.618,
     'L0_conv_bq': 8.0,
     'L0_conv_wk': 6.514,
     'L0_conv_bk': 8.0,
     'L0_conv_bv': 2.812}
    for name, (base, spread) in spreads.items():
        noise = np.random.default_rng([zlib.crc32(name.encode()), seed]).standard_normal(out[name].shape)
        drawn = base * np.exp(spread * noise) if base else spread * noise
        out[name] = jnp.asarray(drawn.astype(out[name].dtype))
    for name, factor in factors.items():
        out[name] = (out[name] * factor).astype(out[name].dtype)
    return out
```

```python
import concourse.bass as bass
from concourse import mybir
from contextlib import ExitStack

BATCH, C, N = 4, 256, 1024
C8, GROUPS = 32, 32
EPS = 1e-5
P = 128
CH = C // P
QC = 512
CHUNKS = N // QC
QT = QC // P
NT = N // P
TILES = CHUNKS * QT

SCORE_0 = ["G.0", "V.0", "V.1", "S0.0", "S0.1", "S0.2", "S0.3", "G.1", "S0.4", "S0.5", "S0.6", "S0.7"]
SCORE_01 = ["G.0", "V.0", "V.1", "S0.0", "XT.0", "S0.1", "XT.1", "S0.2", "FBC", "S0.3", "FD.0", "FD.1",
            "ATT", "S2.0", "S2.1", "S2.2", "S2.3", "G.1", "S0.4", "S0.5", "S0.6", "S0.7",
            "S2.4", "S2.5", "S2.6", "S2.7"]
SCORE_1 = [u for u in SCORE_01 if u not in SCORE_0]


def turns(kind, tiles):
    return [f"{kind}.{t}.{h}" for t in tiles for h in range(2)]


STATS = ["MEAN", "VAR"]
TURN_START = ["MEAN", "VAR"]
TURN_0 = turns("T0", range(8)) + STATS
TURN_01N = (turns("T0", range(4)) + turns("T2", range(3)) + ["ET"] + turns("T2", [3]) + turns("T0", range(4, 8))
            + turns("T2", range(4, 7)) + STATS + turns("T2", [7]))
TURN_01 = [u for u in TURN_01N if u not in STATS]
TURN_1 = turns("T2", range(3)) + ["ET"] + turns("T2", range(3, 8))
SUM_0 = ["O0.0", "O0.1"]
SUM_01 = ["O0.0", "O2.0", "O0.1", "O2.1"]
SUM_1 = ["O2.0", "O2.1"]


class Ring:

    def __init__(self, phases, paired, unstaged=()):
        self.at = []
        self.paired = paired
        used, staged = [0, 0], [0, 0]
        self.start = []
        for names in phases:
            self.start.append((tuple(used), tuple(staged)))
            table = {}
            for n, name in enumerate(names):
                for s in ((0, 1) if paired else (n % 2,)):
                    table[name, s if paired else None] = (s, used[s], staged[s])
                    used[s] += 1
                    staged[s] += name not in unstaged
            self.at.append(table)


class Phase:

    def __init__(self, i, like):
        self.i, self.like = i, like
        self.fixed = isinstance(i, int)

    def count(self, n_like, per_phase):
        if self.fixed:
            return n_like
        return self.i * per_phase + (n_like - self.like * per_phase)

    def slot(self, ring, use, half=None):
        return ring.at[self.like][use, half][0]

    def _nth(self, ring, use, half, what):
        s = self.slot(ring, use, half)
        n = ring.at[self.like][use, half][1 + what]
        a, b = ring.start[LOOP[0]][what][s], ring.start[LOOP[0] + 1][what][s]
        return self.count(n, b - a)

    def uses(self, ring, use, half=None):
        return self._nth(ring, use, half, 0)

    def staged(self, ring, use, half=None):
        return self._nth(ring, use, half, 1)


LOOP = (1, 3)
SCORE = Ring([SCORE_0, SCORE_01, SCORE_01, SCORE_01, SCORE_1], False)
TURN = Ring([TURN_START + TURN_0, TURN_01N, TURN_01N, TURN_01, TURN_1], False, unstaged=STATS)
SUM = Ring([SUM_0, SUM_01, SUM_01, SUM_01, SUM_1], True)


def dual_attention_kernel(nc, x, gn_w, gn_b, wq, bq, wk, bk, wv, bv, wo, bo,
                          wb, bb, wc, bc, wd, bd, alpha, beta, out):
    f32, f32r = mybir.dt.float32, mybir.dt.float32r
    ALU = mybir.AluOpType
    ACT = mybir.ActivationFunctionType
    AX = mybir.AxisListType

    x_dram = x.rearrange("b (m p) h w -> b p m (h w)", p=P)
    out_dram = out.rearrange("b (m p) h w -> b p m (h w)", p=P)

    ctx = ExitStack()
    with ctx:
        def sb(name, shape, dt=f32):
            return ctx.enter_context(nc.sbuf_tensor(name, shape, dt))

        def sem(name):
            return ctx.enter_context(nc.semaphore(name))

        def pair(name):
            return [sem(f"{name}_{s}") for s in range(2)]

        a_w = [sb(f"a_w_{p}", [P, CH, C], f32r) for p in "hl"]
        b_w = [sb(f"b_w_{p}", [P, CH, C], f32r) for p in "hl"]
        d_w = [sb(f"d_w_{p}", [P, CH, C], f32r) for p in "hl"]
        bbc_w = [sb(f"bbc_w_{p}", [P, CH, 3 * C8], f32r) for p in "hl"]
        ident = sb("ident", [P, P])
        group_mean = sb("group_mean", [P, P])
        GN_W, GN_B, BQ, BV, BO, BD, G_BIAS, C_BIAS, ALPHA_BD = range(9)
        vecs = sb("vecs", [P, 9, CH])
        bbc_bias = sb("bbc_bias", [3 * C8, 1])
        gains = sb("gains", [P, 2])

        x_in = sb("x_in", [P, CH, N])
        x1 = sb("x1", [P, CH, N])
        xn_h = sb("xn_h", [P, CH, N], f32r)
        xn_l = sb("xn_l", [P, CH, N], f32r)
        g_h = sb("g_h", [P, CH, QC], f32r)
        g_l = sb("g_l", [P, CH, QC], f32r)
        v_h = sb("v_h", [P, NT, C], f32r)
        v_l = sb("v_l", [P, NT, C], f32r)
        P0_SLOTS, P2_SLOTS = 3, 2
        probs0 = sb("probs0", [P, P0_SLOTS, N])
        probs2 = sb("probs2", [P, P2_SLOTS, N])
        pt0_h = sb("pt0_h", [P, NT, QC], f32r)
        pt0_l = sb("pt0_l", [P, NT, QC], f32r)
        pt2_h = sb("pt2_h", [P, NT, QC], f32r)
        pt2_l = sb("pt2_l", [P, NT, QC], f32r)
        x1_h = sb("x1_h", [P, CH, N], f32r)
        x1_l = sb("x1_l", [P, CH, N], f32r)
        fd_h = sb("fd_h", [P, NT, C], f32r)
        fd_l = sb("fd_l", [P, NT, C], f32r)
        fb_parts = sb("fb_parts", [3 * C8, N], f32r)
        fc_parts = sb("fc_parts", [3 * C8, N], f32r)
        et_h = sb("et_h", [P, CH, C], f32r)
        et_l = sb("et_l", [P, CH, C], f32r)
        out_sb = sb("out_sb", [P, CH, N])
        RUNS = 4
        bn_raw = sb("bn_raw", [P, CH, 2, 6])
        bn_parts = bn_raw[:, :, :, :].rearrange("p m h (e t) -> p (m h e) t", t=3)
        diff, square = sb("diff", [P, CH, RUNS]), sb("square", [P, CH, RUNS])
        spread_sb = sb("spread_sb", [P, CH * RUNS])
        stat = sb("stat", [P, 4, CH])
        GMEAN, VARIANCE, GVAR, RSTD = range(4)
        power = sb("power", [P, CH])
        negmax0, rowsum0, recip0 = (sb(f"{n}0", [P, TILES]) for n in ("negmax", "rowsum", "recip"))
        negmax2, rowsum2, recip2 = (sb(f"{n}2", [P, TILES]) for n in ("negmax", "rowsum", "recip"))
        rowmin_e, rowsum_e, recip_e = (sb(f"{n}_e", [P, CH]) for n in ("rowmin", "rowsum", "recip"))

        xt_h = pt2_h[:, 0:NT // 2, :].rearrange("p a (b c) -> p (a b) c", c=C)
        xt_l = pt2_l[:, 0:NT // 2, :].rearrange("p a (b c) -> p (a b) c", c=C)
        xn = probs0[:, 0:CH, :]
        e_sb = probs0[:, 2, 0:CH * C].rearrange("p (m d) -> p m d", d=C)
        out_flat = out_sb[:, :, :].rearrange("p m n -> p (m n)")

        def in_w(n):
            return out_flat[:, n * CH * C:(n + 1) * CH * C].rearrange("p (m c) -> p m c", c=C)
        wq_sb, wk_sb, wv_sb, wo_sb = (in_w(n) for n in range(4))
        p2_flat = probs2[:, :, :].rearrange("p s n -> p (s n)")
        wd_sb = p2_flat[:, 0:CH * C].rearrange("p (m c) -> p m c", c=C)
        wkg_sb = p2_flat[:, CH * C:2 * CH * C].rearrange("p (m c) -> p m c", c=C)
        wb_sb = p2_flat[0:C8, 2 * CH * C:2 * CH * C + C]
        wc_sb = p2_flat[0:C8, 2 * CH * C + C:2 * CH * C + 2 * C]
        gw_row = p2_flat[:, 2 * CH * C + 2 * C:2 * CH * C + 3 * C]
        x1_flat = x1[:, :, :].rearrange("p m n -> p (m n)")
        wot_sb, a1_sb, b1_sb = (x1_flat[:, n * CH * C:(n + 1) * CH * C].rearrange("p (m c) -> p m c", c=C)
                                for n in range(3))
        as_sb, bs_sb = (probs0[:, 2, n * CH * C:(n + 1) * CH * C].rearrange("p (m c) -> p m c", c=C)
                        for n in range(2))

        score_ps = [ctx.enter_context(nc.psum_tensor(f"score_ps_{s}", [P, 2 * QC], f32)) for s in range(2)]
        turn_ps = [ctx.enter_context(nc.psum_tensor(f"turn_ps_{s}", [P, QC], f32)) for s in range(2)]
        sum_ps = [ctx.enter_context(nc.psum_tensor(f"sum_ps_{s}", [P, QC], f32)) for s in range(2)]

        score_full, score_staged, score_done = pair("score_full"), pair("score_staged"), pair("score_done")
        turn_full, turn_staged, turn_done = pair("turn_full"), pair("turn_staged"), pair("turn_done")
        sum_full, sum_done = pair("sum_full"), pair("sum_done")
        x0_loaded = pair("x0_loaded")
        x_loaded = pair("x_loaded")
        w_loaded = sem("w_loaded")
        wd_loaded = sem("wd_loaded")
        v_loaded = sem("v_loaded")
        out_stored = sem("out_stored")
        consts_made = sem("consts_made")
        xn_made = sem("xn_made")
        xn_high = sem("xn_high")
        xn_split = sem("xn_split")
        x_copied = sem("x_copied")
        probs0_made = sem("probs0_made")
        probs2_made = sem("probs2_made")
        e_made = sem("e_made")
        x1_high = sem("x1_high")
        x1_split = sem("x1_split")
        base_made = sem("base_made")
        recip_made0, recip_made2, recip_made_e = sem("recip_made0"), sem("recip_made2"), sem("recip_made_e")
        bn_made = sem("bn_made")
        rstd_made = sem("rstd_made")
        dve_step = sem("dve_step")
        prep_pe, prep_act, prep_dve = sem("prep_pe"), sem("prep_act"), sem("prep_dve")

        BN_STEPS = 4

        block = ctx.enter_context(nc.Block())

        def phases(eng, body):
            body(Phase(0, 0), True, False, True)
            with eng.Fori(LOOP[0], LOOP[1]) as i:
                body(Phase(i, LOOP[0]), True, True, True)
            body(Phase(BATCH - 1, BATCH - 1), True, True, False)
            body(Phase(BATCH, BATCH), False, True, False)

        def wait(eng, semaphore, count):
            if not (isinstance(count, int) and count == 0):
                eng.wait_ge(semaphore, count)

        @block.sync
        def _(sp):
            for m in range(CH):
                sp.dma_start(x_in[:, m, :], x_dram[0, :, m, :]).then_inc(x0_loaded[m], 16)
            sp.dma_start(wd_sb, wd.rearrange("(m p) c -> p m c", p=P)).then_inc(wd_loaded, 16)
            sp.dma_start(wb_sb, wb).then_inc(wd_loaded, 16)
            sp.dma_start(wc_sb, wc).then_inc(wd_loaded, 16)

        @block.gpsimd
        def _(pool):
            pool.memset(ident[:, :], 0.0).then_inc(consts_made, 1)
            pool.memset(group_mean[:, :], float(GROUPS) / C / RUNS).then_inc(consts_made, 1)
            pool.memset(power[:, :], -0.5).then_inc(consts_made, 1)
            pool.wait_ge(consts_made, 3)
            pool.affine_select(out=ident[:, :], in_=ident[:, :], compare_op=ALU.not_equal, fill=1.0, base=0,
                               pattern=[[-1, P]], channel_multiplier=1).then_inc(consts_made, 1)
            per = C // GROUPS
            blocks = group_mean[:, :].rearrange("p (g c) -> p g c", c=per)
            pool.affine_select(out=blocks, in_=blocks, compare_op=ALU.is_ge, fill=0.0, base=0,
                               pattern=[[-per, P // per], [0, per]], channel_multiplier=1).then_inc(consts_made, 1)
            pool.wait_ge(consts_made, 5)
            pool.affine_select(out=blocks, in_=blocks, compare_op=ALU.is_ge, fill=0.0, base=per - 1,
                               pattern=[[per, P // per], [0, per]], channel_multiplier=-1).then_inc(consts_made, 1)

            def rstd(s, n):
                pool.wait_ge(turn_done[s], n + 1)
                pool.tensor_tensor(stat[:, RSTD, :], stat[:, GVAR, :], power[:, :], ALU.pow)\
                    .then_inc(rstd_made, 1)

            def split_xn(b):
                for m in range(CH):
                    pool.wait_ge(xn_high, b * CH + m + 1)
                    pool.tensor_tensor(xn_l[:, m, :], xn[:, m, :], xn_h[:, m, :].bitcast(f32), ALU.subtract)\
                        .then_inc(xn_split, 1)

            def load(ph):
                b = ph.i + 1
                pool.wait_ge(xn_made, ph.i * CH + CH)
                pool.wait_ge(x_copied, ph.i * (CH * 16) + CH * 16)
                src = x_dram[b] if ph.fixed else x_dram[bass.ds(b, 1)][0]
                for m in range(CH):
                    pool.dma_start(x_in[:, m, :], src[:, m, :])\
                        .then_inc(x_loaded[m], 16)

            def store(ph, c):
                a = ph.i - 1
                dst = out_dram[a] if ph.fixed else out_dram[bass.ds(a, 1)][0]
                for m in range(CH):
                    pool.wait_ge(sum_done[m], ph.uses(SUM, f"O2.{c}", m) + 1)
                    pool.dma_start(dst[:, m, c * QC:(c + 1) * QC], out_sb[:, m, c * QC:(c + 1) * QC])\
                        .then_inc(out_stored, 16)

            rstd(TURN_START.index("VAR"), 0)
            split_xn(0)

            def body(ph, zero, one, more):
                if one:
                    for m in range(CH):
                        pool.wait_ge(x1_high, (ph.i - 1) * CH + (m + 1))
                        pool.tensor_tensor(x1_l[:, m, :], x1[:, m, :], x1_h[:, m, :].bitcast(f32), ALU.subtract)\
                            .then_inc(x1_split, 1)
                if more:
                    load(ph)
                if one:
                    store(ph, 0)
                if more:
                    rstd(ph.slot(TURN, "VAR"), ph.uses(TURN, "VAR"))
                    split_xn(ph.i + 1)
                if one:
                    store(ph, 1)
                    pool.wait_ge(out_stored, ph.i * (16 * CHUNKS * CH))
            phases(pool, body)

        @block.scalar
        def _(act):
            for dst, src in ((wq_sb, wq), (wk_sb, wk), (wv_sb, wv), (wo_sb, wo)):
                act.dma_start(dst, src.rearrange("(m p) c -> p m c", p=P)).then_inc(w_loaded, 16)
            act.dma_start(gw_row, gn_w.rearrange("(a c) -> a c", a=1).broadcast_to([P, C])).then_inc(v_loaded, 16)
            with nc.allow_non_contiguous_dma(reason="vectors of 256 words"):
                for n, v in ((GN_W, gn_w), (GN_B, gn_b), (BQ, bq), (BV, bv), (BO, bo), (BD, bd)):
                    act.dma_start(vecs[:, n, :], v.rearrange("(m p) -> p m", p=P)).then_inc(v_loaded, 16)
            for n, v in enumerate((bb, bb, bc)):
                act.dma_start(bbc_bias[n * C8:(n + 1) * C8, :], v.rearrange("(p a) -> p a", a=1))\
                    .then_inc(v_loaded, 16)
            for n, v in enumerate((alpha, beta)):
                act.dma_start(gains[:, n:n + 1], v.rearrange("(a c) -> a c", a=1).broadcast_to([P, 1]))\
                    .then_inc(v_loaded, 16)

            def high(dst, src, bias=0.0):
                if isinstance(bias, float):
                    return act.activation(dst, src, ACT.Copy)
                return act.activation(dst, src, ACT.Identity, bias=bias)

            def split_xn(b):
                for m in range(CH):
                    act.wait_ge(xn_made, b * CH + (m + 1))
                    high(xn_h[:, m, :], xn[:, m, :]).then_inc(xn_high, 1)

            act.wait_ge(prep_pe, 2)
            high(d_w[0][:, :, :], turn_ps[1][:, :].rearrange("p (m c) -> p m c", c=C)).then_inc(prep_act, 1)
            act.wait_ge(prep_pe, 3)
            high(bbc_w[0][:, :, :], sum_ps[0][:, 0:CH * 3 * C8].rearrange("p (m c) -> p m c", c=3 * C8))\
                .then_inc(prep_act, 1)
            act.wait_ge(prep_pe, 4)
            act.activation(a1_sb, score_ps[0][:, 0:CH * C].rearrange("p (m c) -> p m c", c=C), ACT.Copy)\
                .then_inc(prep_act, 1)
            act.wait_ge(prep_pe, 5)
            act.activation(b1_sb, score_ps[1][:, 0:CH * C].rearrange("p (m c) -> p m c", c=C), ACT.Copy)\
                .then_inc(prep_act, 1)
            act.wait_ge(prep_dve, 5)
            high(a_w[0][:, :, :], as_sb).then_inc(prep_act, 1)
            act.wait_ge(prep_dve, 6)
            high(b_w[0][:, :, :], bs_sb).then_inc(prep_act, 1)
            split_xn(0)

            def stage_score(ph, use, dst, src_of=lambda ps: ps[:, :], bias=0.0):
                s, n = ph.slot(SCORE, use), ph.uses(SCORE, use)
                act.wait_ge(score_full[s], n + 1)
                high(dst, src_of(score_ps[s]), bias).then_inc(score_staged[s], 1)

            def exp_score(ph, use, dst, neg, total):
                s = ph.slot(SCORE, use)
                act.wait_ge(score_staged[s], ph.staged(SCORE, use) + 1)
                act.activation(dst, score_ps[s][:, :], ACT.Exp, bias=neg, scale=1.0, accum_out=total)\
                    .then_inc(score_done[s], 1)

            def exp0(ph, j):
                exp_score(ph, f"S0.{j}", probs0[:, j % P0_SLOTS, :], negmax0[:, j:j + 1], rowsum0[:, j:j + 1])

            def exp2(ph, j):
                exp_score(ph, f"S2.{j}", probs2[:, j % P2_SLOTS, :], negmax2[:, j:j + 1], rowsum2[:, j:j + 1])

            def stage_turn(ph, kind, pt, j):
                jj = j % QT
                for h in range(2):
                    use = f"{kind}.{j}.{h}"
                    s = ph.slot(TURN, use)
                    act.wait_ge(turn_full[s], ph.uses(TURN, use) + 1)
                    high(pt[:, h * 4:(h + 1) * 4, jj * P:(jj + 1) * P],
                         turn_ps[s][:, :].rearrange("p (k q) -> p k q", q=P)).then_inc(turn_staged[s], 1)

            def g_high(ph, c):
                s, n = ph.slot(SCORE, f"G.{c}"), ph.uses(SCORE, f"G.{c}")
                act.wait_ge(score_full[s], n + 1)
                for m in range(CH):
                    last = high(g_h[:, m, :], score_ps[s][:, m * QC:(m + 1) * QC], vecs[:, G_BIAS, m:m + 1])
                last.then_inc(score_staged[s], 1)

            def copy_x(ph, one):
                if one:
                    act.wait_ge(base_made, ph.i * CH)
                else:
                    for m in range(CH):
                        act.wait_ge(x0_loaded[m], 16)
                    act.wait_ge(prep_dve, PREP_DVE)
                    act.wait_ge(prep_pe, PREP_PE)
                for m in range(CH):
                    act.dma_start(x1[:, m, :], x_in[:, m, :]).then_inc(x_copied, 16)

            def body(ph, zero, one, more):
                if one:
                    act.wait_ge(sum_done[1], ph.uses(SUM, "O0.0" if zero else "O2.0", 1))
                    for m in range(CH):
                        high(x1_h[:, m, :], x1[:, m, :]).then_inc(x1_high, 1)
                if zero:
                    g_high(ph, 0)
                    for u in range(2):
                        stage_score(ph, f"V.{u}", v_h[:, 4 * u:4 * u + 4, :],
                                    lambda ps: ps[:, :].rearrange("p (t c) -> p t c", c=C))
                    exp0(ph, 0)
                if one:
                    stage_score(ph, "XT.0", xt_h[:, 0:4, :], lambda ps: ps[:, :].rearrange("p (t c) -> p t c", c=C))
                if zero:
                    exp0(ph, 1)
                    stage_turn(ph, "T0", pt0_h, 0)
                if one:
                    stage_score(ph, "XT.1", xt_h[:, 4:8, :], lambda ps: ps[:, :].rearrange("p (t c) -> p t c", c=C))
                if zero:
                    exp0(ph, 2)
                    stage_turn(ph, "T0", pt0_h, 1)
                if one:
                    s = ph.slot(SCORE, "FBC")
                    act.wait_ge(score_full[s], ph.uses(SCORE, "FBC") + 1)
                    high(fb_parts[0:2 * C8, :], score_ps[s][0:2 * C8, :], bbc_bias[0:2 * C8, :])
                    high(fc_parts[0:C8, :], score_ps[s][2 * C8:3 * C8, :], bbc_bias[2 * C8:3 * C8, :])
                    high(fc_parts[2 * C8:3 * C8, :], score_ps[s][2 * C8:3 * C8, :], bbc_bias[2 * C8:3 * C8, :])\
                        .then_inc(score_staged[s], 1)
                    for m in range(CH):
                        act.activation(out_sb[:, m, :], x1[:, m, :], ACT.Identity, scale=2.0,
                                       bias=vecs[:, ALPHA_BD, m:m + 1]).then_inc(base_made, 1)
                if zero:
                    copy_x(ph, one)
                    exp0(ph, 3)
                    stage_turn(ph, "T0", pt0_h, 2)
                if one:
                    stage_score(ph, "FD.0", fd_h[:, 0:4, :], lambda ps: ps[:, :].rearrange("p (t c) -> p t c", c=C))
                if zero:
                    stage_turn(ph, "T0", pt0_h, 3)
                if one:
                    stage_score(ph, "FD.1", fd_h[:, 4:8, :], lambda ps: ps[:, :].rearrange("p (t c) -> p t c", c=C))
                    s = ph.slot(SCORE, "ATT")
                    act.wait_ge(score_staged[s], ph.staged(SCORE, "ATT") + 1)
                    for m in range(CH):
                        last = act.activation(e_sb[:, m, :], score_ps[s][:, m * C:(m + 1) * C], ACT.Exp,
                                              bias=rowmin_e[:, m:m + 1], scale=-1.0, accum_out=rowsum_e[:, m:m + 1])
                    last.then_inc(score_done[s], 1)
                    for j in range(4):
                        exp2(ph, j)
                        if j:
                            stage_turn(ph, "T2", pt2_h, j - 1)
                    s = ph.slot(TURN, "ET")
                    act.wait_ge(turn_full[s], ph.uses(TURN, "ET") + 1)
                    high(et_h[:, :, :], turn_ps[s][:, :].rearrange("p (m c) -> p m c", c=C))\
                        .then_inc(turn_staged[s], 1)
                if zero:
                    g_high(ph, 1)
                    exp0(ph, 4)
                if one:
                    stage_turn(ph, "T2", pt2_h, 3)
                if zero:
                    for j in range(5, 8):
                        exp0(ph, j)
                        stage_turn(ph, "T0", pt0_h, j - 1)
                    stage_turn(ph, "T0", pt0_h, 7)
                if one:
                    for j in range(4, 8):
                        exp2(ph, j)
                        if j > 4:
                            stage_turn(ph, "T2", pt2_h, j - 1)
                if more:
                    split_xn(ph.i + 1)
                if one:
                    stage_turn(ph, "T2", pt2_h, 7)
            phases(act, body)

        @block.vector
        def _(dve):
            def low(dst, src, high_part, bias=None):
                hp = high_part.bitcast(f32)
                if bias is None:
                    return dve.tensor_tensor(dst, src, hp, ALU.subtract)
                return dve.scalar_tensor_tensor(dst, src, bias, hp, ALU.add, ALU.subtract)

            def link(ins, count):
                ins.then_inc(dve_step, 1)
                dve.wait_ge(dve_step, count)

            def bn_stats(b, later=True):
                for m in range(CH):
                    dve.wait_ge(x_loaded[m] if later else x0_loaded[m], b * 16 if later else 16)
                    for h in range(2):
                        last = dve.bn_stats(out=bn_raw[:, m, h, :], in_=x_in[:, m, h * 512:(h + 1) * 512])
                    last.then_inc(bn_made, 1)

            def spread(ph_or_start, b):
                s, n = stat_use(ph_or_start, "MEAN")
                dve.wait_ge(turn_full[s], n + 1)
                means = bn_parts[:, :, 1].rearrange("p (m r) -> p m r", r=RUNS)
                gmean = stat[:, GMEAN, :]
                link(dve.tensor_reduce(gmean, turn_ps[s][:, 0:CH * RUNS].rearrange("p (m r) -> p m r", r=RUNS),
                                       AX.X, ALU.add), b * BN_STEPS + 1)
                link(dve.tensor_tensor(diff[:, :, :], means, gmean.unsqueeze(2).broadcast_to([P, CH, RUNS]),
                                       ALU.subtract), b * BN_STEPS + 2)
                link(dve.tensor_tensor(square[:, :, :], diff[:, :, :], diff[:, :, :], ALU.mult), b * BN_STEPS + 3)
                dve.scalar_tensor_tensor(spread_sb[:, :], bn_parts[:, :, 2], RUNS / N,
                                         square[:, :, :].rearrange("p m r -> p (m r)"), ALU.mult, ALU.add)\
                    .then_inc(turn_done[s], 1)

            def group_var(ph_or_start, b):
                s, n = stat_use(ph_or_start, "VAR")
                dve.wait_ge(turn_full[s], n + 1)
                link(dve.tensor_reduce(stat[:, VARIANCE, :],
                                       turn_ps[s][:, 0:CH * RUNS].rearrange("p (m r) -> p m r", r=RUNS),
                                       AX.X, ALU.add), b * BN_STEPS + 4)
                dve.tensor_scalar(stat[:, GVAR, :], stat[:, VARIANCE, :], EPS, None, ALU.add)\
                    .then_inc(turn_done[s], 1)

            def make_xn(b):
                dve.wait_ge(rstd_made, b + 1)
                for m in range(CH):
                    dve.tensor_scalar(xn[:, m, :], x_in[:, m, :], stat[:, GMEAN, m:m + 1], stat[:, RSTD, m:m + 1],
                                      ALU.subtract, ALU.mult).then_inc(xn_made, 1)

            def stat_use(ph, use):
                if ph is None:
                    return TURN_START.index(use), 0
                return ph.slot(TURN, use), ph.uses(TURN, use)

            bn_stats(0, later=False)
            dve.wait_ge(w_loaded, 16 * 4)
            dve.wait_ge(v_loaded, 16 * 12)
            for m in range(CH):
                last = dve.scalar_tensor_tensor(wkg_sb[:, m, :], wk_sb[:, m, :], float(C) ** -0.5, gw_row,
                                                ALU.mult, ALU.mult)
            last.then_inc(prep_dve, 1)
            spread(None, 0)
            group_var(None, 0)
            dve.wait_ge(prep_pe, 1)
            dve.tensor_copy(wot_sb, score_ps[0][:, 0:CH * C].rearrange("p (m c) -> p m c", c=C))\
                .then_inc(prep_dve, 1)
            make_xn(0)
            dve.wait_ge(prep_act, 1)
            low(d_w[1][:, :, :], turn_ps[1][:, :].rearrange("p (m c) -> p m c", c=C), d_w[0][:, :, :])\
                .then_inc(prep_dve, 1)
            dve.wait_ge(prep_act, 2)
            low(bbc_w[1][:, :, :], sum_ps[0][:, 0:CH * 3 * C8].rearrange("p (m c) -> p m c", c=3 * C8),
                bbc_w[0][:, :, :]).then_inc(prep_dve, 1)
            for n, (scaled, plain) in enumerate(((as_sb, a1_sb), (bs_sb, b1_sb))):
                dve.wait_ge(prep_act, 3 + n)
                for m in range(CH):
                    last = dve.tensor_scalar(scaled[:, m, :], plain[:, m, :], vecs[:, GN_W, m:m + 1], None, ALU.mult)
                last.then_inc(prep_dve, 1)
            dve.wait_ge(prep_act, 5)
            low(a_w[1][:, :, :], as_sb, a_w[0][:, :, :]).then_inc(prep_dve, 1)
            dve.wait_ge(prep_act, 6)
            low(b_w[1][:, :, :], bs_sb, b_w[0][:, :, :]).then_inc(prep_dve, 1)
            dve.wait_ge(prep_pe, PREP_PE)
            for m in range(CH):
                dve.tensor_copy(vecs[:, G_BIAS, m:m + 1], sum_ps[1][:, m:m + 1])
                dve.tensor_tensor(vecs[:, C_BIAS, m:m + 1], sum_ps[1][:, CH + m:CH + m + 1], vecs[:, BO, m:m + 1],
                                  ALU.add)
            dve.tensor_scalar(vecs[:, ALPHA_BD, :], vecs[:, BD, :], gains[:, 0:1], None, ALU.mult)\
                .then_inc(prep_dve, 1)

            def row_max(ph, use, dst):
                s = ph.slot(SCORE, use)
                dve.wait_ge(score_full[s], ph.uses(SCORE, use) + 1)
                dve.tensor_reduce(dst, score_ps[s][:, :], AX.X, ALU.max, negate=True).then_inc(score_staged[s], 1)

            def max0(ph, j):
                row_max(ph, f"S0.{j}", negmax0[:, j:j + 1])

            def max2(ph, j):
                row_max(ph, f"S2.{j}", negmax2[:, j:j + 1])

            def norm0(ph, j):
                s = ph.slot(SCORE, f"S0.{j}")
                dve.wait_ge(score_done[s], ph.uses(SCORE, f"S0.{j}") + 1)
                dve.reciprocal(recip0[:, j:j + 1], rowsum0[:, j:j + 1]).then_inc(recip_made0, 1)
                dve.wait_ge(recip_made0, ph.i * TILES + (j + 1))
                slot = probs0[:, j % P0_SLOTS, :]
                dve.tensor_scalar(slot, slot, recip0[:, j:j + 1], None, ALU.mult).then_inc(probs0_made, 1)

            def norm2(ph, j):
                s = ph.slot(SCORE, f"S2.{j}")
                dve.wait_ge(score_done[s], ph.uses(SCORE, f"S2.{j}") + 1)
                dve.reciprocal(recip2[:, j:j + 1], rowsum2[:, j:j + 1]).then_inc(recip_made2, 1)
                dve.wait_ge(recip_made2, (ph.i - 1) * TILES + (j + 1))
                slot = probs2[:, j % P2_SLOTS, :]
                dve.tensor_scalar(slot, slot, recip2[:, j:j + 1], gains[:, 0:1], ALU.mult, ALU.mult)\
                    .then_inc(probs2_made, 1)

            def low_score(ph, use, dst, high_part):
                s = ph.slot(SCORE, use)
                dve.wait_ge(score_staged[s], ph.staged(SCORE, use) + 1)
                low(dst, score_ps[s][:, :].rearrange("p (t c) -> p t c", c=C), high_part)\
                    .then_inc(score_done[s], 1)

            def low_g(ph, c):
                s = ph.slot(SCORE, f"G.{c}")
                dve.wait_ge(score_staged[s], ph.staged(SCORE, f"G.{c}") + 1)
                for m in range(CH):
                    last = low(g_l[:, m, :], score_ps[s][:, m * QC:(m + 1) * QC], g_h[:, m, :],
                               vecs[:, G_BIAS, m:m + 1])
                last.then_inc(score_done[s], 1)

            def low_turn(ph, kind, pt, pt_high, j):
                jj = j % QT
                for h in range(2):
                    use = f"{kind}.{j}.{h}"
                    s = ph.slot(TURN, use)
                    dve.wait_ge(turn_staged[s], ph.staged(TURN, use) + 1)
                    low(pt[:, h * 4:(h + 1) * 4, jj * P:(jj + 1) * P],
                        turn_ps[s][:, :].rearrange("p (k q) -> p k q", q=P),
                        pt_high[:, h * 4:(h + 1) * 4, jj * P:(jj + 1) * P]).then_inc(turn_done[s], 1)

            def low0(ph, j):
                low_turn(ph, "T0", pt0_l, pt0_h, j)

            def low2(ph, j):
                low_turn(ph, "T2", pt2_l, pt2_h, j)

            def body(ph, zero, one, more):
                def finish_x1(c):
                    for m in range(CH):
                        if c == 0 and m == 0:
                            dve.wait_ge(x_copied, ph.i * (CH * 16) + CH * 16)
                        dve.wait_ge(sum_full[m], ph.uses(SUM, f"O0.{c}", m) + 1)
                        part = x1[:, m, c * QC:(c + 1) * QC]
                        dve.scalar_tensor_tensor(part, sum_ps[m][:, :], vecs[:, C_BIAS, m:m + 1], part,
                                                 ALU.add, ALU.add).then_inc(sum_done[m], 1)

                def finish_out(c):
                    for m in range(CH):
                        if c == 0:
                            dve.wait_ge(base_made, (ph.i - 1) * CH + (m + 1))
                        dve.wait_ge(sum_full[m], ph.uses(SUM, f"O2.{c}", m) + 1)
                        part = out_sb[:, m, c * QC:(c + 1) * QC]
                        dve.tensor_tensor(part, sum_ps[m][:, :], part, ALU.add).then_inc(sum_done[m], 1)

                if zero:
                    low_g(ph, 0)
                    for u in range(2):
                        low_score(ph, f"V.{u}", v_l[:, 4 * u:4 * u + 4, :], v_h[:, 4 * u:4 * u + 4, :])
                    max0(ph, 0)
                if one:
                    low_score(ph, "XT.0", xt_l[:, 0:4, :], xt_h[:, 0:4, :])
                if zero:
                    norm0(ph, 0)
                    max0(ph, 1)
                    low0(ph, 0)
                if one:
                    low_score(ph, "XT.1", xt_l[:, 4:8, :], xt_h[:, 4:8, :])
                if zero:
                    norm0(ph, 1)
                    max0(ph, 2)
                    low0(ph, 1)
                if one:
                    s = ph.slot(SCORE, "FBC")
                    dve.wait_ge(score_staged[s], ph.staged(SCORE, "FBC") + 1)
                    low(fb_parts[2 * C8:3 * C8, :], score_ps[s][0:C8, :], fb_parts[0:C8, :], bbc_bias[0:C8, :])
                    low(fc_parts[C8:2 * C8, :], score_ps[s][2 * C8:3 * C8, :], fc_parts[2 * C8:3 * C8, :],
                        bbc_bias[2 * C8:3 * C8, :]).then_inc(score_done[s], 1)
                if zero:
                    norm0(ph, 2)
                    max0(ph, 3)
                    low0(ph, 2)
                    norm0(ph, 3)
                if one:
                    low_score(ph, "FD.0", fd_l[:, 0:4, :], fd_h[:, 0:4, :])
                if zero:
                    low0(ph, 3)
                if one:
                    low_score(ph, "FD.1", fd_l[:, 4:8, :], fd_h[:, 4:8, :])
                    s = ph.slot(SCORE, "ATT")
                    dve.wait_ge(score_full[s], ph.uses(SCORE, "ATT") + 1)
                    dve.tensor_reduce(rowmin_e[:, :], score_ps[s][:, 0:CH * C].rearrange("p (m d) -> p m d", d=C),
                                      AX.X, ALU.min).then_inc(score_staged[s], 1)
                    max2(ph, 0)
                    dve.wait_ge(score_done[s], ph.uses(SCORE, "ATT") + 1)
                    dve.reciprocal(recip_e[:, :], rowsum_e[:, :]).then_inc(recip_made_e, 1)
                    dve.wait_ge(recip_made_e, ph.i)
                    for m in range(CH):
                        dve.tensor_scalar(e_sb[:, m, :], e_sb[:, m, :], recip_e[:, m:m + 1], gains[:, 1:2],
                                          ALU.mult, ALU.mult).then_inc(e_made, 1)
                    norm2(ph, 0)
                    for j in range(1, 4):
                        max2(ph, j)
                        low2(ph, j - 1)
                        norm2(ph, j)
                    s = ph.slot(TURN, "ET")
                    dve.wait_ge(turn_staged[s], ph.staged(TURN, "ET") + 1)
                    low(et_l[:, :, :], turn_ps[s][:, :].rearrange("p (m c) -> p m c", c=C), et_h[:, :, :])\
                        .then_inc(turn_done[s], 1)
                if zero:
                    finish_x1(0)
                    low_g(ph, 1)
                    max0(ph, 4)
                if one:
                    low2(ph, 3)
                if zero:
                    norm0(ph, 4)
                    for j in range(5, 8):
                        max0(ph, j)
                        low0(ph, j - 1)
                        norm0(ph, j)
                    low0(ph, 7)
                if one:
                    finish_out(0)
                if more:
                    bn_stats(ph.i + 1)
                if one:
                    max2(ph, 4)
                    for j in range(5, 8):
                        norm2(ph, j - 1)
                        max2(ph, j)
                        low2(ph, j - 1)
                    norm2(ph, 7)
                if more:
                    spread(ph, ph.i + 1)
                    group_var(ph, ph.i + 1)
                if zero:
                    finish_x1(1)
                if more:
                    make_xn(ph.i + 1)
                if one:
                    low2(ph, 7)
                    finish_out(1)
            phases(dve, body)

        @block.tensor
        def _(pe):
            def product(dst, lhs, rhs, start, stop):
                pe.matmul(dst, lhs[0], rhs[0], start=start, stop=False)
                pe.matmul(dst, lhs[0], rhs[1], start=False, stop=False)
                return pe.matmul(dst, lhs[1], rhs[0], start=False, stop=stop)

            pe.wait_ge(consts_made, 6)

            def group_average(s, n, src, ready, count):
                pe.wait_ge(ready, count)
                if not (isinstance(n, int) and n == 0):
                    pe.wait_ge(turn_done[s], n)
                pe.matmul(turn_ps[s][:, 0:CH * RUNS], group_mean[:, :], src, start=True, stop=True)\
                    .then_inc(turn_full[s], 1)

            pe.wait_ge(w_loaded, 16 * 4)
            for oh in range(CH):
                for m in range(CH):
                    last = pe.transpose(score_ps[0][:, oh * C + m * P:oh * C + (m + 1) * P],
                                        wo_sb[:, m, oh * P:(oh + 1) * P], ident[:, :])
            last.then_inc(prep_pe, 1)
            group_average(0, 0, bn_parts[:, :, 1], bn_made, CH)
            group_average(1, 0, spread_sb[:, :], turn_done[0], 1)
            pe.wait_ge(wd_loaded, 16 * 3)
            pe.wait_ge(turn_done[1], 1)
            for ih in range(CH):
                for m in range(CH):
                    last = pe.transpose(turn_ps[1][:, ih * C + m * P:ih * C + (m + 1) * P],
                                        wd_sb[:, m, ih * P:(ih + 1) * P], ident[:, :])
            last.then_inc(prep_pe, 1)
            for ih in range(CH):
                for n, w in enumerate((wb_sb, wb_sb, wc_sb)):
                    at = (ih * 3 + n) * C8
                    last = pe.transpose(sum_ps[0][:, at:at + C8], w[:, ih * P:(ih + 1) * P], ident[0:C8, 0:C8])
            last.then_inc(prep_pe, 1)
            pe.wait_ge(prep_dve, 2)
            for m in range(CH):
                for oh in range(CH):
                    last = pe.matmul(score_ps[0][:, m * C:(m + 1) * C], wq_sb[:, oh, m * P:(m + 1) * P],
                                     wkg_sb[:, oh, :], start=(oh == 0), stop=(oh == CH - 1))
            last.then_inc(prep_pe, 1)
            for m in range(CH):
                for oh in range(CH):
                    last = pe.matmul(score_ps[1][:, m * C:(m + 1) * C], wv_sb[:, oh, m * P:(m + 1) * P],
                                     wot_sb[:, oh, :], start=(oh == 0), stop=(oh == CH - 1))
            last.then_inc(prep_pe, 1)
            pe.wait_ge(v_loaded, 16 * 12)
            pe.wait_ge(prep_act, 4)
            for m in range(CH):
                for n, (w, v) in enumerate(((a1_sb, GN_B), (wkg_sb, BQ))):
                    for oh in range(CH):
                        pe.matmul(sum_ps[1][:, m:m + 1], w[:, oh, m * P:(m + 1) * P], vecs[:, v, oh:oh + 1],
                                  start=(n == 0 and oh == 0), stop=(n == 1 and oh == CH - 1))
            for m in range(CH):
                for n, (w, v) in enumerate(((b1_sb, GN_B), (wot_sb, BV))):
                    for oh in range(CH):
                        last = pe.matmul(sum_ps[1][:, CH + m:CH + m + 1], w[:, oh, m * P:(m + 1) * P],
                                         vecs[:, v, oh:oh + 1], start=(n == 0 and oh == 0),
                                         stop=(n == 1 and oh == CH - 1))
            last.then_inc(prep_pe, 1)
            pe.wait_ge(prep_dve, PREP_DVE)

            def enter(ph, use):
                s = ph.slot(SCORE, use)
                wait(pe, score_done[s], ph.uses(SCORE, use))
                return s, score_ps[s]

            def after(ph, use):
                s = ph.slot(SCORE, use)
                pe.wait_ge(score_done[s], ph.uses(SCORE, use) + 1)

            def cols(t, n=P):
                return slice(t * n, (t + 1) * n)

            def both(parts, *index):
                return [p[index] for p in parts]

            xn_p, g_p, v_p, x1_p, fd_p = (xn_h, xn_l), (g_h, g_l), (v_h, v_l), (x1_h, x1_l), (fd_h, fd_l)
            pt0_p, pt2_p, xt_p, et_p = (pt0_h, pt0_l), (pt2_h, pt2_l), (xt_h, xt_l), (et_h, et_l)
            every = slice(None)

            def project_g(ph, c):
                s, ps = enter(ph, f"G.{c}")
                for m in range(CH):
                    for k in range(CH):
                        last = product(ps[:, cols(m, QC)], both(a_w, every, k, cols(m)),
                                       both(xn_p, every, k, cols(c, QC)), k == 0, k == CH - 1)
                last.then_inc(score_full[s], 1)

            def project_rows(ph, use, u, data, w):
                s, ps = enter(ph, use)
                for t in range(4):
                    for k in range(CH):
                        last = product(ps[:, cols(t, C)], both(data, every, k, cols(4 * u + t)),
                                       both(w, every, k, every), k == 0, k == CH - 1)
                last.then_inc(score_full[s], 1)

            def scores0(ph, j):
                s, ps = enter(ph, f"S0.{j}")
                for n in range(2):
                    for k in range(CH):
                        last = product(ps[:, cols(n, QC)], both(g_p, every, k, cols(j % QT)),
                                       both(xn_p, every, k, cols(n, QC)), k == 0, k == CH - 1)
                last.then_inc(score_full[s], 1)

            def scores2(ph, j):
                s, ps = enter(ph, f"S2.{j}")
                for n in range(2):
                    last = pe.matmul(ps[:, cols(n, QC)], fb_parts[:, cols(j)], fc_parts[:, cols(n, QC)],
                                     start=True, stop=True)
                last.then_inc(score_full[s], 1)

            def turn(ph, kind, ring_sb, slots, j, made, count):
                pe.wait_ge(made, count)
                for h in range(2):
                    use = f"{kind}.{j}.{h}"
                    s = ph.slot(TURN, use)
                    wait(pe, turn_done[s], ph.uses(TURN, use))
                    for t in range(4):
                        last = pe.transpose(turn_ps[s][:, cols(t)], ring_sb[:, j % slots, cols(4 * h + t)],
                                            ident[:, :])
                    last.then_inc(turn_full[s], 1)

            def turn0(ph, j):
                turn(ph, "T0", probs0, P0_SLOTS, j, probs0_made, ph.i * TILES + (j + 1))

            def turn2(ph, j):
                turn(ph, "T2", probs2, P2_SLOTS, j, probs2_made, (ph.i - 1) * TILES + (j + 1))

            def turned(ph, use):
                s = ph.slot(TURN, use)
                pe.wait_ge(turn_done[s], ph.uses(TURN, use) + 1)

            def sum_steps(ph, kind, c):
                v, pt = (v_p, pt0_p) if kind == "O0" else (fd_p, pt2_p)
                for m in range(CH):
                    wait(pe, sum_done[m], ph.uses(SUM, f"{kind}.{c}", m))
                    if kind == "O2":
                        for k in range(CH):
                            product(sum_ps[m][:, :], both(et_p, every, k, cols(m)),
                                    both(x1_p, every, k, cols(c, QC)), k == 0, False)
                    for k in range(NT):
                        last = product(sum_ps[m][:, :], both(v, every, k, cols(m)), both(pt, every, k, every),
                                       kind == "O0" and k == 0, k == NT - 1)
                        if k == NT - 1:
                            last.then_inc(sum_full[m], 1)
                        yield

            def stats(ph, use):
                s = ph.slot(TURN, use)
                if use == "MEAN":
                    group_average(s, ph.uses(TURN, use), bn_parts[:, :, 1], bn_made, ph.i * CH + 2 * CH)
                else:
                    m = ph.slot(TURN, "MEAN")
                    group_average(s, ph.uses(TURN, use), spread_sb[:, :], turn_done[m],
                                  ph.uses(TURN, "MEAN") + 1)

            def run(gen, steps=None):
                n = 0
                for _ in gen:
                    n += 1
                    if n == steps:
                        return

            def body(ph, zero, one, more):
                a = ph.i - 1
                if zero:
                    pe.wait_ge(xn_split, ph.i * CH + CH)
                    project_g(ph, 0)
                    for u in range(2):
                        project_rows(ph, f"V.{u}", u, xn_p, b_w)
                    after(ph, "G.0")
                    scores0(ph, 0)
                if one:
                    pe.wait_ge(sum_done[1], ph.uses(SUM, "O0.0" if zero else "O2.0", 1))
                for j in range(2):
                    if one:
                        s, ps = enter(ph, f"XT.{j}")
                        for t in range(4):
                            for k in range(CH):
                                last = pe.transpose(ps[:, t * C + k * P:t * C + (k + 1) * P],
                                                    x1[:, k, cols(4 * j + t)], ident[:, :])
                        last.then_inc(score_full[s], 1)
                    if zero:
                        scores0(ph, j + 1)
                        turn0(ph, j)
                if one:
                    pe.wait_ge(x1_split, ph.i * CH)
                    s, ps = enter(ph, "FBC")
                    for n in range(2):
                        for k in range(CH):
                            last = product(ps[0:3 * C8, cols(n, QC)], both(bbc_w, every, k, every),
                                           both(x1_p, every, k, cols(n, QC)), k == 0, k == CH - 1)
                    last.then_inc(score_full[s], 1)
                if zero:
                    scores0(ph, 3)
                    turn0(ph, 2)
                if one:
                    project_rows(ph, "FD.0", 0, x1_p, d_w)
                if zero:
                    turn0(ph, 3)
                if one:
                    project_rows(ph, "FD.1", 1, x1_p, d_w)
                    after(ph, "XT.1")
                    s, ps = enter(ph, "ATT")
                    for m in range(CH):
                        for t in range(NT):
                            last = product(ps[:, cols(m, C)], both(xt_p, every, t, cols(m)),
                                           both(xt_p, every, t, every), t == 0, t == NT - 1)
                    last.then_inc(score_full[s], 1)
                    after(ph, "FBC")

                def channel_turn():
                    pe.wait_ge(e_made, ph.i * CH)
                    s = ph.slot(TURN, "ET")
                    wait(pe, turn_done[s], ph.uses(TURN, "ET"))
                    for dh in range(CH):
                        for m in range(CH):
                            last = pe.transpose(turn_ps[s][:, dh * C + m * P:dh * C + (m + 1) * P],
                                                e_sb[:, m, cols(dh)], ident[:, :])
                    last.then_inc(turn_full[s], 1)

                if zero:
                    after(ph, "V.0")
                    after(ph, "V.1")
                    turned(ph, "T0.3.1")
                    sums = sum_steps(ph, "O0", 0)
                for j in range(4):
                    if one:
                        scores2(ph, j)
                    if zero:
                        run(sums, 4)
                    if one and j:
                        turn2(ph, j - 1)
                if one:
                    channel_turn()
                if zero:
                    run(sums)
                    project_g(ph, 1)
                    if one:
                        turn2(ph, 3)
                    after(ph, "G.1")
                    scores0(ph, 4)
                    for j in range(5, 8):
                        scores0(ph, j)
                        turn0(ph, j - 1)
                elif one:
                    turn2(ph, 3)
                if one:
                    turned(ph, "ET")
                    turned(ph, "T2.3.1")
                    after(ph, "FD.0")
                    after(ph, "FD.1")
                    sums = sum_steps(ph, "O2", 0)
                    run(sums, 4)
                if zero:
                    turn0(ph, 7)
                if one:
                    run(sums)
                if zero:
                    turned(ph, "T0.7.1")
                    sums = sum_steps(ph, "O0", 1)
                for j in range(4, 8):
                    if one:
                        scores2(ph, j)
                    if zero:
                        run(sums, 4)
                    if one and j > 4:
                        turn2(ph, j - 1)
                if more:
                    stats(ph, "MEAN")
                    stats(ph, "VAR")
                if zero:
                    run(sums)
                if one:
                    turn2(ph, 7)
                    turned(ph, "T2.7.1")
                    run(sum_steps(ph, "O2", 1))
            phases(pe, body)


PREP_DVE, PREP_PE = 9, 6

_INS = ["x"] + [f"L0_conv_{n}" for n in ("gn_w", "gn_b", "wq", "bq", "wk", "bk", "wv", "bv", "wo", "bo")] \
    + [f"L1_conv_{n}" for n in ("wb", "bb", "wc", "bc", "wd", "bd", "alpha", "beta")]
_OUTS = [((BATCH, C, 32, 32), "float32")]


def kernel(**inputs):
    import numpy as _np
    import concourse.bacc as _bacc
    from concourse import mybir as _mybir
    from concourse.bass_utils import run_bass_kernel_spmd as _run

    nc = _bacc.Bacc("TRN2", target_bir_lowering=False, num_devices=1)
    arrays, args = {}, []
    for name in _INS:
        a = _np.ascontiguousarray(inputs[name])
        arrays[f"in_{name}_dram"] = a
        args.append(nc.dram_tensor(f"in_{name}_dram", a.shape, _mybir.dt.from_np(a.dtype), kind="ExternalInput").ap())
    for i, (shape, dtype) in enumerate(_OUTS):
        dt = _mybir.dt.from_np(_np.dtype(dtype))
        args.append(nc.dram_tensor(f"out_{i}_dram", shape, dt, kind="ExternalOutput").ap())
    dual_attention_kernel(nc, *args)
    r = _run(nc, [arrays], core_ids=[0])
    return r.results[0]["out_0_dram"]
```

```python
import concourse.bass as bass
from concourse import mybir
from contextlib import ExitStack

BATCH, C, N = 4, 256, 1024
C8, GROUPS = 32, 32
EPS = 1e-5
P = 128
CH = C // P
QC = 512
CHUNKS = N // QC
QT = QC // P
NT = N // P
TILES = CHUNKS * QT

PE_FIRST = """
    G.0 BG W V.0 S0.0 S0.1 S0.2 T0.0.0 T0.0.1 S0.3 T0.1.0 G.1 T0.1.1 V.1 MEAN T0.2.0 VAR T0.2.1 T0.3.0 S0.4
    T0.3.1 S0.5 S0.6 T0.4.0 S0.7 T0.4.1 O0.0x2 T0.5.0 O0.0x1 T0.5.1 O0.0x6 T0.6.0 T0.6.1 O0.0x2 T0.7.0 T0.7.1
    O0.0x5 O0.1x16
""".split()
PE_STEADY = """
    G.0 V.0 XT.0 XT.1 S0.0 S0.1 S0.2 T0.0.0 T0.0.1 S0.3 T0.1.0 T0.1.1 G.1 V.1 T0.2.0 T0.2.1 S0.4 T0.3.0 T0.3.1
    FBC ATT O0.0x1 S2.0 O0.0x2 S2.1 O0.0x2 FD.0 T2.0.0 T2.0.1 O0.0x2 S2.2 FD.1 T2.1.0 O0.0x1 T2.1.1 O0.0x2
    S2.3 O0.0x2 MEAN O0.0x3 VAR ET S0.5 T2.2.0 T2.2.1 S0.6 O0.0x1 T2.3.0 T2.3.1 O2.0x2 T0.4.0 O2.0x2 S2.4
    T0.4.1 O2.0x1 T0.5.0 S0.7 O2.0x2 T0.5.1 S2.5 O2.0x4 T0.6.0 T0.6.1 O2.0x2 T0.7.0 O2.0x3 T0.7.1 O2.0x2
    T2.4.0 T2.4.1 S2.6 O0.1x3 T2.5.0 O0.1x2 T2.5.1 S2.7 O0.1x5 T2.6.0 O0.1x3 T2.6.1 O0.1x3 T2.7.0 T2.7.1
    O2.1x18
""".split()
PE_LAST = """
    XT.0 p:O2.1x2 XT.1 p:O2.1x2 FBC p:O2.1x1 ATT p:O2.1x1 S2.0 S2.1 p:O2.1x2 ET S2.2 T2.0.0 S2.3 T2.0.1 FD.0
    T2.1.0 T2.1.1 FD.1 T2.2.0 T2.2.1 S2.4 O2.0x1 T2.3.0 T2.3.1 O2.0x1 S2.5 S2.6 O2.0x2 T2.4.0 T2.4.1 O2.0x2
    S2.7 O2.0x2 T2.5.0 O2.0x3 T2.5.1 O2.0x3 T2.6.0 T2.6.1 O2.0x4 T2.7.0 T2.7.1 O2.1x18
""".split()
ACT_FIRST = """
    hG.0 hV.0 xcopyI exp0.0 exp0.1 hT0.0.0 exp0.2 hT0.0.1 hT0.1.0 hW exp0.3 hT0.1.1 hG.1 hT0.2.0 hV.1 hT0.2.1
    hT0.3.0 exp0.4 exp0.5 hT0.3.1 hT0.4.0 hT0.4.1 exp0.6 hT0.5.0 exp0.7 hT0.5.1 hT0.6.0 hT0.6.1 hT0.7.0
    hT0.7.1 xnh.0 xnh.1 x1h.0 x1h.1
""".split()
ACT_STEADY = """
    hG.0 hV.0 hXT.0 hXT.1 exp0.0 exp0.1 hT0.0.0 exp0.2 hT0.0.1 hT0.1.0 hT0.1.1 exp0.3 hG.1 hV.1 hT0.2.0
    hT0.2.1 hT0.3.0 exp0.4 hT0.3.1 hFBC base.0 base.1 xcopyI expE exp2.0 exp2.1 hFD.0 hT2.0.0 hT2.0.1 hFD.1
    hT2.1.0 exp2.2 hT2.1.1 hET exp2.3 hT2.2.0 hT2.2.1 exp0.5 hT2.3.0 hT2.3.1 hT0.4.0 exp0.6 hT0.4.1 hT0.5.0
    exp2.4 hT0.5.1 exp0.7 hT0.6.0 hT0.6.1 exp2.5 hT0.7.0 hT0.7.1 hT2.4.0 hT2.4.1 hT2.5.0 exp2.6 hT2.5.1 exp2.7
    hT2.6.0 hT2.6.1 hT2.7.0 hT2.7.1 xnh.0 x1h.0 xnh.1 x1h.1
""".split()
ACT_LAST = """
    hXT.0 hXT.1 hFBC expE exp2.0 exp2.1 hET hT2.0.0 exp2.2 hT2.0.1 exp2.3 hT2.1.0 hT2.1.1 hFD.0 hT2.2.0
    hT2.2.1 hFD.1 hT2.3.0 hT2.3.1 exp2.4 exp2.5 hT2.4.0 hT2.4.1 base.0 exp2.6 hT2.5.0 exp2.7 hT2.5.1 base.1
    hT2.6.0 hT2.6.1 hT2.7.0 hT2.7.1
""".split()
DVE_FIRST = """
    lG.0 lV.0 max0.0 max0.1 norm0.0 max0.2 lT0.0.0 norm0.1 norm0.2 max0.3 lT0.0.1 bn lT0.1.0 lT0.1.1 norm0.3
    spread lT0.2.0 gvar lG.1 lV.1 lT0.2.1 lT0.3.0 max0.4 lW norm0.4 max0.5 lT0.3.1 lT0.4.0 norm0.5 lT0.4.1
    max0.6 max0.7 norm0.6 lT0.5.0 norm0.7 lT0.5.1 lT0.6.0 lT0.6.1 xn.0 lT0.7.0 lT0.7.1 fx.0.0 fx.0.1 xn.1
    fx.1.0 fx.1.1
""".split()
DVE_STEADY = """
    lG.0 lV.0 lXT.0 lXT.1 max0.0 norm0.0 max0.1 max0.2 norm0.1 lT0.0.0 lT0.0.1 max0.3 lT0.1.0 lT0.1.1 norm0.2
    norm0.3 lG.1 lV.1 lT0.2.0 lT0.2.1 max0.4 norm0.4 lT0.3.0 lT0.3.1 lFBC minE max2.0 norm2.0 max2.1 nE
    norm2.1 lFD.0 lT2.0.0 max2.2 lT2.0.1 bn lT2.1.0 lFD.1 spread lT2.1.1 norm2.2 gvar max2.3 lET fx.0.0 max0.5
    lT2.2.0 norm2.3 lT2.2.1 max0.6 fx.0.1 lT2.3.0 lT2.3.1 lT0.4.0 norm0.5 max2.4 lT0.4.1 lT0.5.0 norm0.6
    max0.7 lT0.5.1 norm2.4 max2.5 norm0.7 lT0.6.0 norm2.5 lT0.6.1 fo.0.0 lT0.7.0 lT0.7.1 fo.0.1 lT2.4.0 xn.0
    max2.6 lT2.4.1 lT2.5.0 max2.7 lT2.5.1 norm2.6 fx.1.0 norm2.7 lT2.6.0 lT2.6.1 fx.1.1 lT2.7.0 lT2.7.1 xn.1
    fo.1.0 fo.1.1
""".split()
DVE_LAST = """
    lXT.0 lXT.1 p:fo.1.0 lFBC minE max2.0 nE max2.1 norm2.0 max2.2 lET max2.3 lT2.0.0 norm2.1 lT2.0.1 p:fo.1.1
    norm2.2 lT2.1.0 lT2.1.1 lFD.0 norm2.3 lT2.2.0 lT2.2.1 max2.4 lFD.1 lT2.3.0 lT2.3.1 norm2.4 max2.5 max2.6
    norm2.5 lT2.4.0 max2.7 lT2.4.1 norm2.6 norm2.7 lT2.5.0 lT2.5.1 fo.0.0 lT2.6.0 lT2.6.1 fo.0.1 lT2.7.0
    lT2.7.1 fo.1.0 fo.1.1
""".split()
POOL_FIRST = """
    loadI rstd xnl.0 xnl.1 x1l.0 x1l.1
""".split()
POOL_STEADY = """
    loadI rstd x1l.0 xnl.0 xnl.1 stI.0.0 x1l.1 stI.0.1 stI.1.0 stI.1.1 st.1
""".split()
POOL_LAST = """
    p:stI.1.0 p:stI.1.1 p:st.1
""".split()
NEXT_BATCH = {"loadI", "bn", "MEAN", "spread", "VAR", "gvar", "rstd", "xn", "xnh", "xnl"}
STATS = ["MEAN", "VAR"]
CARRIED = 8
C_BIAS_AT = 256
SCORE_KINDS = {"G", "V", "S0", "XT", "FBC", "FD", "ATT", "S2"}
TURN_KINDS = {"T0", "T2", "ET", "MEAN", "VAR"}


def kind(step):
    return step.split(".")[0]


def without_next(steps):
    return [s for s in steps if kind(s) not in NEXT_BATCH]


def without_carried(steps):
    steps, left = [s for s in steps if s not in ("fo.1.0", "fo.1.1", "stI.1.0", "stI.1.1", "st.1")], CARRIED
    for n in range(len(steps) - 1, -1, -1):
        if steps[n].startswith("O2.1x") and left:
            here = int(steps[n][len("O2.1x"):])
            steps[n] = f"O2.1x{max(here - left, 0)}"
            left = max(left - here, 0)
    return [s for s in steps if s != "O2.1x0"]


def per_phase(first, steady, last):
    return [first, steady, steady, without_carried(without_next(steady)), last]


def uses_of(kinds, steps):
    return [s for s in steps if kind(s) in kinds]


def sums_of(steps):
    return list(dict.fromkeys(s.split("x")[0] for s in steps if s[0] == "O"))


class Ring:

    def __init__(self, phases, paired, unstaged=()):
        self.at = []
        self.paired = paired
        used, staged = [0, 0], [0, 0]
        self.start = []
        for names in phases:
            self.start.append((tuple(used), tuple(staged)))
            table = {}
            for n, name in enumerate(names):
                for s in ((0, 1) if paired else (n % 2,)):
                    table[name, s if paired else None] = (s, used[s], staged[s])
                    used[s] += 1
                    staged[s] += name not in unstaged
            self.at.append(table)


class Phase:

    def __init__(self, i, like):
        self.i, self.like = i, like
        self.fixed = isinstance(i, int)
        self.zero, self.one = like < BATCH, like > 0

    def count(self, n_like, per_phase):
        if self.fixed:
            return n_like
        return self.i * per_phase + (n_like - self.like * per_phase)

    def slot(self, ring, use, half=None):
        return ring.at[self.like][use, half][0]

    def _nth(self, ring, use, half, what):
        s = self.slot(ring, use, half)
        n = ring.at[self.like][use, half][1 + what]
        a, b = ring.start[LOOP[0]][what][s], ring.start[LOOP[0] + 1][what][s]
        return self.count(n, b - a)

    def uses(self, ring, use, half=None):
        return self._nth(ring, use, half, 0)

    def staged(self, ring, use, half=None):
        return self._nth(ring, use, half, 1)

    def last_uses(self, ring, uses):
        at = ring.at[self.like]
        return {at[u, None][0]: u for u in sorted(uses, key=lambda u: at[u, None][1])}.values()


LOOP = (1, 3)
PE_PHASES = per_phase(PE_FIRST, PE_STEADY, PE_LAST)
ACT_PHASES = per_phase(ACT_FIRST, ACT_STEADY, ACT_LAST)
DVE_PHASES = per_phase(DVE_FIRST, DVE_STEADY, DVE_LAST)
POOL_PHASES = per_phase(POOL_FIRST, POOL_STEADY, POOL_LAST)
SCORE = Ring([uses_of(SCORE_KINDS, steps) for steps in PE_PHASES], False)
TURN = Ring([STATS + uses_of(TURN_KINDS, PE_PHASES[0])] + [uses_of(TURN_KINDS, steps) for steps in PE_PHASES[1:]],
            False, unstaged=STATS)
SUM = Ring([sums_of(steps) for steps in PE_PHASES], True)


def dual_attention_kernel(nc, x, gn_w, gn_b, wq, bq, wk, bk, wv, bv, wo, bo,
                          wb, bb, wc, bc, wd, bd, alpha, beta, out):
    f32, f32r = mybir.dt.float32, mybir.dt.float32r
    ALU = mybir.AluOpType
    ACT = mybir.ActivationFunctionType
    AX = mybir.AxisListType

    x_dram = x.rearrange("b (m p) h w -> b p m (h w)", p=P)
    out_dram = out.rearrange("b (m p) h w -> b p m (h w)", p=P)

    ctx = ExitStack()
    with ctx:
        def sb(name, shape, dt=f32):
            return ctx.enter_context(nc.sbuf_tensor(name, shape, dt))

        def sem(name):
            return ctx.enter_context(nc.semaphore(name))

        def pair(name):
            return [sem(f"{name}_{s}") for s in range(2)]

        a_w = [sb(f"a_w_{p}", [P, CH, C], f32r) for p in "hl"]
        b_w = [sb(f"b_w_{p}", [P, CH, C], f32r) for p in "hl"]
        d_w = [sb(f"d_w_{p}", [P, CH, C], f32r) for p in "hl"]
        bbc_w = [sb(f"bbc_w_{p}", [P, CH, 3 * C8], f32r) for p in "hl"]
        ident = sb("ident", [P, P])
        group_mean = sb("group_mean", [P, P])
        GN_W, GN_B, BQ, BV, BO, BD, G_BIAS, C_BIAS, ALPHA_BD = range(9)
        vecs = sb("vecs", [P, 9, CH])
        bbc_bias = sb("bbc_bias", [3 * C8, 1])
        gains = sb("gains", [P, 2])

        x_in = sb("x_in", [P, CH, N])
        x1 = sb("x1", [P, CH, N])
        xn_h = sb("xn_h", [P, CH, N], f32r)
        xn_l = sb("xn_l", [P, CH, N], f32r)
        g_h = sb("g_h", [P, CH, QC], f32r)
        g_l = sb("g_l", [P, CH, QC], f32r)
        v_h = sb("v_h", [P, NT, C], f32r)
        v_l = sb("v_l", [P, NT, C], f32r)
        probs0 = sb("probs0", [P, 3, N])
        probs2 = sb("probs2", [P, 2, N])
        pt0_h = sb("pt0_h", [P, NT, QC], f32r)
        pt0_l = sb("pt0_l", [P, NT, QC], f32r)
        pt2_h = sb("pt2_h", [P, NT, QC], f32r)
        pt2_l = sb("pt2_l", [P, NT, QC], f32r)
        x1_h = sb("x1_h", [P, CH, N], f32r)
        x1_l = sb("x1_l", [P, CH, N], f32r)
        fd_h = sb("fd_h", [P, NT, C], f32r)
        fd_l = sb("fd_l", [P, NT, C], f32r)
        fb_parts = sb("fb_parts", [3 * C8, N], f32r)
        fc_parts = sb("fc_parts", [3 * C8, N], f32r)
        et_h = sb("et_h", [P, CH, C], f32r)
        et_l = sb("et_l", [P, CH, C], f32r)
        out_sb = sb("out_sb", [P, CH, N])
        RUNS = 4
        bn_raw = sb("bn_raw", [P, CH, 2, 6])
        bn_parts = bn_raw[:, :, :, :].rearrange("p m h (e t) -> p (m h e) t", t=3)
        diff, square = sb("diff", [P, CH, RUNS]), sb("square", [P, CH, RUNS])
        spread_sb = sb("spread_sb", [P, CH * RUNS])
        stat = sb("stat", [P, 4, CH])
        GMEAN, VARIANCE, GVAR, RSTD = range(4)
        power = sb("power", [P, CH])
        negmax0, rowsum0, recip0 = (sb(f"{n}0", [P, TILES]) for n in ("negmax", "rowsum", "recip"))
        negmax2, rowsum2, recip2 = (sb(f"{n}2", [P, TILES]) for n in ("negmax", "rowsum", "recip"))
        rowmin_e, rowsum_e, recip_e = (sb(f"{n}_e", [P, CH]) for n in ("rowmin", "rowsum", "recip"))

        xt_h = pt2_h[:, 0:NT // 2, :].rearrange("p a (b c) -> p (a b) c", c=C)
        xt_l = pt2_l[:, 0:NT // 2, :].rearrange("p a (b c) -> p (a b) c", c=C)
        xn = probs0[:, 0:CH, :]
        e_sb = probs0[:, 2, 0:CH * C].rearrange("p (m d) -> p m d", d=C)
        out_flat = out_sb[:, :, :].rearrange("p m n -> p (m n)")

        def in_w(n):
            return out_flat[:, n * CH * C:(n + 1) * CH * C].rearrange("p (m c) -> p m c", c=C)
        wq_sb, wk_sb, wv_sb, wo_sb = (in_w(n) for n in range(4))
        p2_flat = probs2[:, :, :].rearrange("p s n -> p (s n)")
        wd_sb = p2_flat[:, 0:CH * C].rearrange("p (m c) -> p m c", c=C)
        wkg_sb = p2_flat[:, CH * C:2 * CH * C].rearrange("p (m c) -> p m c", c=C)
        wb_sb = p2_flat[0:C8, 2 * CH * C:2 * CH * C + C]
        wc_sb = p2_flat[0:C8, 2 * CH * C + C:2 * CH * C + 2 * C]
        gw_row = p2_flat[:, 2 * CH * C + 2 * C:2 * CH * C + 3 * C]
        x1_flat = x1[:, :, :].rearrange("p m n -> p (m n)")
        wot_sb, a1_sb, b1_sb = (x1_flat[:, n * CH * C:(n + 1) * CH * C].rearrange("p (m c) -> p m c", c=C)
                                for n in range(3))

        def probs_of(ph, block, j):
            if block == "0":
                ring = [probs0[:, n, :] for n in range(3)] + ([] if ph.one else [probs2[:, 0, :]])
            else:
                ring = [probs2[:, n, :] for n in range(2)] + ([] if ph.zero else [probs0[:, n, :] for n in range(2)])
            return ring[j % len(ring)]

        def turned_of(ph, block, c):
            other = c == 1 and not (ph.one and ph.zero)
            return (pt0_h, pt0_l) if (block == "0") != other else (pt2_h, pt2_l)

        score_ps = [ctx.enter_context(nc.psum_tensor(f"score_ps_{s}", [P, 2 * QC], f32)) for s in range(2)]
        turn_ps = [ctx.enter_context(nc.psum_tensor(f"turn_ps_{s}", [P, QC], f32)) for s in range(2)]
        sum_ps = [ctx.enter_context(nc.psum_tensor(f"sum_ps_{s}", [P, QC], f32)) for s in range(2)]

        a_ps, b_ps = (ps[:, QC:2 * QC] for ps in score_ps)

        score_full, score_staged, score_done = pair("score_full"), pair("score_staged"), pair("score_done")
        turn_full, turn_staged, turn_done = pair("turn_full"), pair("turn_staged"), pair("turn_done")
        sum_full, sum_done = pair("sum_full"), pair("sum_done")
        x0_loaded = pair("x0_loaded")
        x_loaded = pair("x_loaded")
        wk_loaded = sem("wk_loaded")
        wq_loaded, wo_loaded, wv_loaded = sem("wq_loaded"), sem("wo_loaded"), sem("wv_loaded")
        block1_loaded = sem("block1_loaded")
        gn_w_loaded = sem("gn_w_loaded")
        g_vecs_loaded = sem("g_vecs_loaded")
        vecs_loaded = sem("vecs_loaded")
        out_stored = sem("out_stored")
        last_stored = sem("last_stored")
        out_free = sem("out_free")
        x1_read = sem("x1_read")
        consts_made = sem("consts_made")
        xn_made = sem("xn_made")
        xn_high = sem("xn_high")
        xn_split = sem("xn_split")
        x_copied = sem("x_copied")
        probs0_made = sem("probs0_made")
        probs2_made = sem("probs2_made")
        e_made = sem("e_made")
        x1_high = sem("x1_high")
        x1_split = sem("x1_split")
        base_made = sem("base_made")
        recip_made0, recip_made2, recip_made_e = sem("recip_made0"), sem("recip_made2"), sem("recip_made_e")
        bn_made = sem("bn_made")
        rstd_made = sem("rstd_made")
        dve_step = sem("dve_step")
        wot_turned, wot_made = sem("wot_turned"), sem("wot_made")
        wkg_made = sem("wkg_made")
        a_full, a_high, a_copied, a_made = (sem(f"a_{n}") for n in ("full", "high", "copied", "made"))
        b_full, b_high, b_copied, b_made = (sem(f"b_{n}") for n in ("full", "high", "copied", "made"))
        g_bias_full, g_bias_made = sem("g_bias_full"), sem("g_bias_made")
        rest_full, rest_high, rest_made = sem("rest_full"), sem("rest_high"), sem("rest_made")
        x0_low = sem("x0_low")

        XN = CH * CHUNKS
        BN_STEPS = 4

        block = ctx.enter_context(nc.Block())

        def phases(eng, steps, run_step):
            def body(ph):
                for step in steps[ph.like]:
                    at = ph
                    if step.startswith("p:"):
                        at, step = Phase(ph.i - 1, ph.like - 1), step[2:]
                    name, *numbers = step.replace("x", ".x").split(".") if step[0] == "O" else step.split(".")
                    run_step(at, name, *numbers)
            body(Phase(0, 0))
            with eng.Fori(LOOP[0], LOOP[1]) as i:
                body(Phase(i, LOOP[0]))
            body(Phase(BATCH - 1, BATCH - 1))
            body(Phase(BATCH, BATCH))

        def rows_of(flat):
            return flat.rearrange("p (m c) -> p m c", c=C)

        def wait(eng, semaphore, count):
            if not (isinstance(count, int) and count == 0):
                eng.wait_ge(semaphore, count)

        @block.sync
        def _(sp):
            def load_w(dst, src, semaphore):
                sp.dma_start(dst, src.rearrange("(m p) c -> p m c", p=P)).then_inc(semaphore, 16)

            def load_v(n, v, semaphore):
                with nc.allow_non_contiguous_dma(reason="vectors of 256 words"):
                    sp.dma_start(vecs[:, n, :], v.rearrange("(m p) -> p m", p=P)).then_inc(semaphore, 16)

            for m in range(CH):
                sp.dma_start(x_in[:, m, :], x_dram[0, :, m, :]).then_inc(x0_loaded[m], 16)
            load_w(wo_sb, wo, wo_loaded)
            load_w(wv_sb, wv, wv_loaded)
            load_v(GN_B, gn_b, g_vecs_loaded)
            load_v(BQ, bq, g_vecs_loaded)
            load_w(wd_sb, wd, block1_loaded)
            sp.dma_start(wb_sb, wb).then_inc(block1_loaded, 16)
            sp.dma_start(wc_sb, wc).then_inc(block1_loaded, 16)
            for n, v in ((BV, bv), (BO, bo), (BD, bd)):
                load_v(n, v, vecs_loaded)
            for n, v in enumerate((bb, bb, bc)):
                sp.dma_start(bbc_bias[n * C8:(n + 1) * C8, :], v.rearrange("(p a) -> p a", a=1))\
                    .then_inc(vecs_loaded, 16)
            for n, v in enumerate((alpha, beta)):
                sp.dma_start(gains[:, n:n + 1], v.rearrange("(a c) -> a c", a=1).broadcast_to([P, 1]))\
                    .then_inc(vecs_loaded, 16)

            last = Phase(BATCH, BATCH)
            for c in range(CHUNKS):
                part = slice(c * QC, (c + 1) * QC)
                for m in range(CH):
                    sp.wait_ge(sum_done[m], last.uses(SUM, f"O2.{c}", m) + 1)
                    sp.dma_start(out_dram[BATCH - 1, :, m, part], out_sb[:, m, part]).then_inc(last_stored, 16)
            sp.wait_ge(last_stored, 16 * CHUNKS * CH)

        @block.gpsimd
        def _(pool):
            pool.memset(ident[:, :], 0.0).then_inc(consts_made, 1)
            pool.memset(group_mean[:, :], float(GROUPS) / C / RUNS).then_inc(consts_made, 1)
            pool.memset(power[:, :], -0.5).then_inc(consts_made, 1)
            pool.wait_ge(consts_made, 3)
            pool.affine_select(out=ident[:, :], in_=ident[:, :], compare_op=ALU.not_equal, fill=1.0, base=0,
                               pattern=[[-1, P]], channel_multiplier=1).then_inc(consts_made, 1)
            per = C // GROUPS
            blocks = group_mean[:, :].rearrange("p (g c) -> p g c", c=per)
            pool.affine_select(out=blocks, in_=blocks, compare_op=ALU.is_ge, fill=0.0, base=0,
                               pattern=[[-per, P // per], [0, per]], channel_multiplier=1).then_inc(consts_made, 1)
            pool.wait_ge(consts_made, 5)
            pool.affine_select(out=blocks, in_=blocks, compare_op=ALU.is_ge, fill=0.0, base=per - 1,
                               pattern=[[per, P // per], [0, per]], channel_multiplier=-1).then_inc(consts_made, 1)

            def rstd(s, n):
                pool.wait_ge(turn_done[s], n + 1)
                pool.tensor_tensor(stat[:, RSTD, :], stat[:, GVAR, :], power[:, :], ALU.pow)\
                    .then_inc(rstd_made, 1)

            def split_xn(b, m):
                pool.wait_ge(xn_high, b * XN + (m + 1) * CHUNKS)
                pool.tensor_tensor(xn_l[:, m, :], xn[:, m, :], xn_h[:, m, :].bitcast(f32), ALU.subtract)\
                    .then_inc(xn_split, CHUNKS)

            def split_x1(ph, m):
                pool.wait_ge(x1_high, ph.i * CH + (m + 1))
                pool.tensor_tensor(x1_l[:, m, :], x1[:, m, :], x1_h[:, m, :].bitcast(f32), ALU.subtract)\
                    .then_inc(x1_split, 1)

            def load(ph):
                b = ph.i + 1
                pool.wait_ge(xn_made, ph.i * XN + XN)
                pool.wait_ge(x_copied, ph.i * (CH * 16) + CH * 16)
                src = x_dram[b] if ph.fixed else x_dram[bass.ds(b, 1)][0]
                for m in range(CH):
                    pool.dma_start(x_in[:, m, :], src[:, m, :])\
                        .then_inc(x_loaded[m], 16)

            def store(ph, c, m):
                a = ph.i - 1
                dst = out_dram[a] if ph.fixed else out_dram[bass.ds(a, 1)][0]
                pool.wait_ge(sum_done[m], ph.uses(SUM, f"O2.{c}", m) + 1)
                pool.dma_start(dst[:, m, c * QC:(c + 1) * QC], out_sb[:, m, c * QC:(c + 1) * QC])\
                    .then_inc(out_stored, 16)

            rstd(STATS.index("VAR"), 0)
            late = slice(QC, N)
            for m in range(CH):
                pool.wait_ge(xn_high, CH + (m + 1))
                pool.tensor_tensor(xn_l[:, m, late], xn[:, m, late], xn_h[:, m, late].bitcast(f32), ALU.subtract)\
                    .then_inc(xn_split, CHUNKS)
            pool.sem_inc(out_free, 1)

            def step(ph, name, *numbers):
                n = [int(x) for x in numbers]
                if name == "loadI":
                    load(ph)
                elif name == "stI":
                    store(ph, *n)
                elif name == "st":
                    pool.wait_ge(out_stored, ph.i * (16 * CHUNKS * CH))
                    pool.sem_inc(out_free, 1)
                elif name == "rstd":
                    rstd(ph.slot(TURN, "VAR"), ph.uses(TURN, "VAR"))
                elif name == "xnl":
                    split_xn(ph.i + 1, *n)
                elif name == "x1l":
                    split_x1(ph, *n)
            phases(pool, POOL_PHASES, step)

        @block.scalar
        def _(act):
            act.dma_start(wk_sb, wk.rearrange("(m p) c -> p m c", p=P)).then_inc(wk_loaded, 16)
            act.dma_start(gw_row, gn_w.rearrange("(a c) -> a c", a=1).broadcast_to([P, C])).then_inc(wk_loaded, 16)
            act.dma_start(wq_sb, wq.rearrange("(m p) c -> p m c", p=P)).then_inc(wq_loaded, 16)
            with nc.allow_non_contiguous_dma(reason="a vector of 256 words"):
                act.dma_start(vecs[:, GN_W, :], gn_w.rearrange("(m p) -> p m", p=P)).then_inc(gn_w_loaded, 16)

            def high(dst, src, bias=0.0):
                if isinstance(bias, float):
                    return act.activation(dst, src, ACT.Copy)
                return act.activation(dst, src, ACT.Identity, bias=bias)

            def split_xn(b, m):
                act.wait_ge(xn_made, b * XN + (m + 1) * CHUNKS)
                high(xn_h[:, m, :], xn[:, m, :]).then_inc(xn_high, CHUNKS)

            act.wait_ge(wot_turned, 1)
            act.activation(wot_sb, rows_of(sum_ps[0][:, :]), ACT.Copy).then_inc(wot_made, 1)
            for n, (c, m) in enumerate((c, m) for c in range(CHUNKS) for m in range(CH)):
                part = slice(c * QC, (c + 1) * QC)
                act.wait_ge(xn_made, n + 1)
                high(xn_h[:, m, part], xn[:, m, part]).then_inc(xn_high, 1)
            act.wait_ge(gn_w_loaded, 16)
            for ps, w, full, staged in ((a_ps, a_w, a_full, a_high), (b_ps, b_w, b_full, b_high)):
                act.wait_ge(full, 1)
                for m in range(CH):
                    last = act.activation(w[0][:, m, :], ps[:, m * C:(m + 1) * C], ACT.Copy,
                                          scale=vecs[:, GN_W, m:m + 1])
                last.then_inc(staged, 1)
            for ps, plain, made, copied in ((a_ps, a1_sb, a_made, a_copied), (b_ps, b1_sb, b_made, b_copied)):
                act.wait_ge(made, 1)
                act.activation(plain, rows_of(ps), ACT.Copy).then_inc(copied, 1)

            def rest():
                act.wait_ge(vecs_loaded, 16 * 8)
                act.wait_ge(rest_full, 1)
                act.activation(d_w[0][:, :, :], rows_of(sum_ps[0][:, :]), ACT.Copy, scale=gains[:, 0:1])
                high(bbc_w[0][:, :, :], sum_ps[1][:, 0:CH * 3 * C8].rearrange("p (m c) -> p m c", c=3 * C8))\
                    .then_inc(rest_high, 1)

            def stage_score(ph, use, dst, src_of=lambda ps: ps[:, :], bias=0.0):
                s, n = ph.slot(SCORE, use), ph.uses(SCORE, use)
                act.wait_ge(score_full[s], n + 1)
                high(dst, src_of(score_ps[s]), bias).then_inc(score_staged[s], 1)

            def exp_score(ph, use, dst, neg, total):
                s = ph.slot(SCORE, use)
                act.wait_ge(score_staged[s], ph.staged(SCORE, use) + 1)
                act.activation(dst, score_ps[s][:, :], ACT.Exp, bias=neg, scale=1.0, accum_out=total)\
                    .then_inc(score_done[s], 1)

            def normalise(ph, block, j):
                recip, recip_made, made, before = (recip0, recip_made0, probs0_made, ph.i) if block == "0" else \
                    (recip2, recip_made2, probs2_made, ph.i - 1)
                act.wait_ge(recip_made, before * TILES + (j + 1))
                rows = probs_of(ph, block, j)
                act.activation(rows, rows, ACT.Copy, scale=recip[:, j:j + 1]).then_inc(made, 1)

            def stage_turn(ph, block, j, h):
                use = f"T{block}.{j}.{h}"
                s = ph.slot(TURN, use)
                pt, jj = turned_of(ph, block, j // QT)[0], j % QT
                act.wait_ge(turn_full[s], ph.uses(TURN, use) + 1)
                high(pt[:, h * 4:(h + 1) * 4, jj * P:(jj + 1) * P],
                     turn_ps[s][:, :].rearrange("p (k q) -> p k q", q=P)).then_inc(turn_staged[s], 1)

            def g_high(ph, c):
                s, n = ph.slot(SCORE, f"G.{c}"), ph.uses(SCORE, f"G.{c}")
                act.wait_ge(score_full[s], n + 1)
                if ph.like == 0:
                    act.wait_ge(g_bias_made, 1)
                for m in range(CH):
                    last = high(g_h[:, m, :], score_ps[s][:, m * QC:(m + 1) * QC], vecs[:, G_BIAS, m:m + 1])
                last.then_inc(score_staged[s], 1)

            def copy_x(ph):
                if ph.one:
                    for use in ph.last_uses(SCORE, ["XT.0", "XT.1"]):
                        act.wait_ge(score_full[ph.slot(SCORE, use)], ph.uses(SCORE, use) + 1)
                    act.wait_ge(x1_split, ph.i * CH)
                    act.wait_ge(base_made, ph.i * CH)
                else:
                    for m in range(CH):
                        act.wait_ge(x0_loaded[m], 16)
                    act.wait_ge(rest_full, 1)
                for m in range(CH):
                    act.dma_start(x1[:, m, :], x_in[:, m, :]).then_inc(x_copied, 16)

            def exp_e(ph):
                s = ph.slot(SCORE, "ATT")
                act.wait_ge(score_staged[s], ph.staged(SCORE, "ATT") + 1)
                for m in range(CH):
                    last = act.activation(e_sb[:, m, :], score_ps[s][:, m * C:(m + 1) * C], ACT.Exp,
                                          bias=rowmin_e[:, m:m + 1], scale=-1.0, accum_out=rowsum_e[:, m:m + 1])
                last.then_inc(score_done[s], 1)

            def fbc_high(ph):
                s = ph.slot(SCORE, "FBC")
                act.wait_ge(score_full[s], ph.uses(SCORE, "FBC") + 1)
                high(fb_parts[0:2 * C8, :], score_ps[s][0:2 * C8, :], bbc_bias[0:2 * C8, :])
                high(fc_parts[0:C8, :], score_ps[s][2 * C8:3 * C8, :], bbc_bias[2 * C8:3 * C8, :])
                high(fc_parts[2 * C8:3 * C8, :], score_ps[s][2 * C8:3 * C8, :], bbc_bias[2 * C8:3 * C8, :])\
                    .then_inc(score_staged[s], 1)

            def as_rows(ps):
                return ps[:, :].rearrange("p (t c) -> p t c", c=C)

            def step(ph, name, *numbers):
                n = [int(x) for x in numbers]
                if name == "hG":
                    g_high(ph, *n)
                elif name == "hW":
                    rest()
                elif name in ("hV", "hXT", "hFD"):
                    dst = {"hV": v_h, "hXT": xt_h, "hFD": fd_h}[name]
                    stage_score(ph, f"{name[1:]}.{n[0]}", dst[:, 4 * n[0]:4 * n[0] + 4, :], as_rows)
                elif name in ("exp0", "exp2"):
                    j, block = n[0], name[3]
                    neg, total = (negmax0, rowsum0) if block == "0" else (negmax2, rowsum2)
                    exp_score(ph, f"S{block}.{j}", probs_of(ph, block, j), neg[:, j:j + 1], total[:, j:j + 1])
                elif name in ("norm0", "norm2"):
                    normalise(ph, name[4], *n)
                elif name in ("hT0", "hT2"):
                    stage_turn(ph, name[2], *n)
                elif name == "hFBC":
                    fbc_high(ph)
                elif name == "base":
                    act.wait_ge(out_free, ph.i)
                    act.activation(out_sb[:, n[0], :], x1[:, n[0], :], ACT.Identity, scale=2.0,
                                   bias=vecs[:, ALPHA_BD, n[0]:n[0] + 1]).then_inc(base_made, 1)
                elif name == "xcopyI":
                    copy_x(ph)
                elif name == "expE":
                    exp_e(ph)
                elif name == "hET":
                    s = ph.slot(TURN, "ET")
                    act.wait_ge(turn_full[s], ph.uses(TURN, "ET") + 1)
                    high(et_h[:, :, :], as_rows(turn_ps[s])).then_inc(turn_staged[s], 1)
                elif name == "xnh":
                    act.wait_ge(score_full[ph.slot(SCORE, "S0.7")], ph.uses(SCORE, "S0.7") + 1)
                    split_xn(ph.i + 1, *n)
                elif name == "x1h":
                    for m in range(CH):
                        act.wait_ge(sum_done[m], ph.uses(SUM, "O0.1", m) + 1)
                    if ph.one:
                        act.wait_ge(x1_read, ph.i)
                    high(x1_h[:, n[0], :], x1[:, n[0], :]).then_inc(x1_high, 1)
            phases(act, ACT_PHASES, step)

        @block.vector
        def _(dve):
            def low(dst, src, high_part, bias=None):
                hp = high_part.bitcast(f32)
                if bias is None:
                    return dve.tensor_tensor(dst, src, hp, ALU.subtract)
                return dve.scalar_tensor_tensor(dst, src, bias, hp, ALU.add, ALU.subtract)

            def link(ins, count):
                ins.then_inc(dve_step, 1)
                dve.wait_ge(dve_step, count)

            def bn_stats(b, later=True):
                for m in range(CH):
                    dve.wait_ge(x_loaded[m] if later else x0_loaded[m], b * 16 if later else 16)
                    for h in range(2):
                        last = dve.bn_stats(out=bn_raw[:, m, h, :], in_=x_in[:, m, h * 512:(h + 1) * 512])
                    last.then_inc(bn_made, 1)

            def spread(ph_or_start, b):
                s, n = stat_use(ph_or_start, "MEAN")
                dve.wait_ge(turn_full[s], n + 1)
                means = bn_parts[:, :, 1].rearrange("p (m r) -> p m r", r=RUNS)
                gmean = stat[:, GMEAN, :]
                link(dve.tensor_reduce(gmean, turn_ps[s][:, 0:CH * RUNS].rearrange("p (m r) -> p m r", r=RUNS),
                                       AX.X, ALU.add), b * BN_STEPS + 1)
                link(dve.tensor_tensor(diff[:, :, :], means, gmean.unsqueeze(2).broadcast_to([P, CH, RUNS]),
                                       ALU.subtract), b * BN_STEPS + 2)
                link(dve.tensor_tensor(square[:, :, :], diff[:, :, :], diff[:, :, :], ALU.mult), b * BN_STEPS + 3)
                dve.scalar_tensor_tensor(spread_sb[:, :], bn_parts[:, :, 2], RUNS / N,
                                         square[:, :, :].rearrange("p m r -> p (m r)"), ALU.mult, ALU.add)\
                    .then_inc(turn_done[s], 1)

            def group_var(ph_or_start, b):
                s, n = stat_use(ph_or_start, "VAR")
                dve.wait_ge(turn_full[s], n + 1)
                link(dve.tensor_reduce(stat[:, VARIANCE, :],
                                       turn_ps[s][:, 0:CH * RUNS].rearrange("p (m r) -> p m r", r=RUNS),
                                       AX.X, ALU.add), b * BN_STEPS + 4)
                dve.tensor_scalar(stat[:, GVAR, :], stat[:, VARIANCE, :], EPS, None, ALU.add)\
                    .then_inc(turn_done[s], 1)

            def normalised(m, part):
                return dve.tensor_scalar(xn[:, m, part], x_in[:, m, part], stat[:, GMEAN, m:m + 1],
                                         stat[:, RSTD, m:m + 1], ALU.subtract, ALU.mult)

            def make_xn(b, m):
                dve.wait_ge(rstd_made, b + 1)
                normalised(m, slice(0, N)).then_inc(xn_made, CHUNKS)

            def stat_use(ph, use):
                if ph is None:
                    return STATS.index(use), 0
                return ph.slot(TURN, use), ph.uses(TURN, use)

            bn_stats(0, later=False)
            dve.wait_ge(wk_loaded, 16 * 2)
            for m in range(CH):
                last = dve.scalar_tensor_tensor(wkg_sb[:, m, :], wk_sb[:, m, :], float(C) ** -0.5, gw_row,
                                                ALU.mult, ALU.mult)
            last.then_inc(wkg_made, 1)
            spread(None, 0)
            group_var(None, 0)
            dve.wait_ge(rstd_made, 1)
            for c in range(CHUNKS):
                for m in range(CH):
                    normalised(m, slice(c * QC, (c + 1) * QC)).then_inc(xn_made, 1)
            for m in range(CH):
                dve.wait_ge(xn_high, m + 1)
                last = low(xn_l[:, m, 0:QC], xn[:, m, 0:QC], xn_h[:, m, 0:QC])
            last.then_inc(x0_low, 1)
            dve.wait_ge(gn_w_loaded, 16)
            for ps, w, staged, made in ((a_ps, a_w, a_high, a_made), (b_ps, b_w, b_high, b_made)):
                dve.wait_ge(staged, 1)
                for m in range(CH):
                    last = dve.scalar_tensor_tensor(w[1][:, m, :], ps[:, m * C:(m + 1) * C],
                                                    vecs[:, GN_W, m:m + 1], w[0][:, m, :].bitcast(f32),
                                                    ALU.mult, ALU.subtract)
                last.then_inc(made, 1)
            dve.wait_ge(g_bias_full, 1)
            dve.tensor_copy(vecs[:, G_BIAS, :], turn_ps[0][:, 0:CH]).then_inc(g_bias_made, 1)

            def rest():
                dve.wait_ge(vecs_loaded, 16 * 8)
                dve.wait_ge(rest_high, 1)
                dve.scalar_tensor_tensor(d_w[1][:, :, :], rows_of(sum_ps[0][:, :]), gains[:, 0:1],
                                         d_w[0][:, :, :].bitcast(f32), ALU.mult, ALU.subtract)
                low(bbc_w[1][:, :, :], sum_ps[1][:, 0:CH * 3 * C8].rearrange("p (m c) -> p m c", c=3 * C8),
                    bbc_w[0][:, :, :])
                dve.tensor_scalar(vecs[:, ALPHA_BD, :], vecs[:, BD, :], gains[:, 0:1], None, ALU.mult)
                dve.tensor_tensor(vecs[:, C_BIAS, :], sum_ps[1][:, C_BIAS_AT:C_BIAS_AT + CH], vecs[:, BO, :], ALU.add)\
                    .then_inc(rest_made, 1)

            def row_max(ph, use, dst):
                s = ph.slot(SCORE, use)
                dve.wait_ge(score_full[s], ph.uses(SCORE, use) + 1)
                dve.tensor_reduce(dst, score_ps[s][:, :], AX.X, ALU.max, negate=True).then_inc(score_staged[s], 1)

            def reciprocal(ph, block, j):
                use = f"S{block}.{j}"
                s = ph.slot(SCORE, use)
                rowsum, recip, recip_made = (rowsum0, recip0, recip_made0) if block == "0" else \
                    (rowsum2, recip2, recip_made2)
                dve.wait_ge(score_done[s], ph.uses(SCORE, use) + 1)
                dve.reciprocal(recip[:, j:j + 1], rowsum[:, j:j + 1]).then_inc(recip_made, 1)

            def normalise(ph, block, j):
                reciprocal(ph, block, j)
                recip, recip_made, made, before = (recip0, recip_made0, probs0_made, ph.i) if block == "0" else \
                    (recip2, recip_made2, probs2_made, ph.i - 1)
                dve.wait_ge(recip_made, before * TILES + (j + 1))
                rows = probs_of(ph, block, j)
                dve.tensor_scalar(rows, rows, recip[:, j:j + 1], None, ALU.mult).then_inc(made, 1)

            def low_score(ph, use, dst, high_part):
                s = ph.slot(SCORE, use)
                dve.wait_ge(score_staged[s], ph.staged(SCORE, use) + 1)
                low(dst, score_ps[s][:, :].rearrange("p (t c) -> p t c", c=C), high_part)\
                    .then_inc(score_done[s], 1)

            def low_g(ph, c):
                s = ph.slot(SCORE, f"G.{c}")
                dve.wait_ge(score_staged[s], ph.staged(SCORE, f"G.{c}") + 1)
                for m in range(CH):
                    last = low(g_l[:, m, :], score_ps[s][:, m * QC:(m + 1) * QC], g_h[:, m, :],
                               vecs[:, G_BIAS, m:m + 1])
                last.then_inc(score_done[s], 1)

            def low_turn(ph, block, j, h):
                use = f"T{block}.{j}.{h}"
                s = ph.slot(TURN, use)
                (pt_h, pt_l), jj = turned_of(ph, block, j // QT), j % QT
                dve.wait_ge(turn_staged[s], ph.staged(TURN, use) + 1)
                low(pt_l[:, h * 4:(h + 1) * 4, jj * P:(jj + 1) * P],
                    turn_ps[s][:, :].rearrange("p (k q) -> p k q", q=P),
                    pt_h[:, h * 4:(h + 1) * 4, jj * P:(jj + 1) * P]).then_inc(turn_done[s], 1)

            def low_fbc(ph):
                s = ph.slot(SCORE, "FBC")
                dve.wait_ge(score_staged[s], ph.staged(SCORE, "FBC") + 1)
                low(fb_parts[2 * C8:3 * C8, :], score_ps[s][0:C8, :], fb_parts[0:C8, :], bbc_bias[0:C8, :])
                low(fc_parts[C8:2 * C8, :], score_ps[s][2 * C8:3 * C8, :], fc_parts[2 * C8:3 * C8, :],
                    bbc_bias[2 * C8:3 * C8, :]).then_inc(score_done[s], 1)

            def min_e(ph):
                s = ph.slot(SCORE, "ATT")
                dve.wait_ge(score_full[s], ph.uses(SCORE, "ATT") + 1)
                dve.tensor_reduce(rowmin_e[:, :], score_ps[s][:, 0:CH * C].rearrange("p (m d) -> p m d", d=C),
                                  AX.X, ALU.min).then_inc(score_staged[s], 1)

            def normalise_e(ph):
                s = ph.slot(SCORE, "ATT")
                dve.wait_ge(score_done[s], ph.uses(SCORE, "ATT") + 1)
                dve.reciprocal(recip_e[:, :], rowsum_e[:, :]).then_inc(recip_made_e, 1)
                dve.wait_ge(recip_made_e, ph.i)
                for m in range(CH):
                    dve.tensor_scalar(e_sb[:, m, :], e_sb[:, m, :], recip_e[:, m:m + 1], gains[:, 1:2],
                                      ALU.mult, ALU.mult).then_inc(e_made, 1)

            def finish_x1(ph, c, m):
                dve.wait_ge(x_copied, ph.i * (CH * 16) + CH * 16)
                dve.wait_ge(sum_full[m], ph.uses(SUM, f"O0.{c}", m) + 1)
                part = x1[:, m, c * QC:(c + 1) * QC]
                dve.scalar_tensor_tensor(part, sum_ps[m][:, :], vecs[:, C_BIAS, m:m + 1], part,
                                         ALU.add, ALU.add).then_inc(sum_done[m], 1)

            def finish_out(ph, c, m):
                dve.wait_ge(base_made, (ph.i - 1) * CH + (m + 1))
                dve.wait_ge(sum_full[m], ph.uses(SUM, f"O2.{c}", m) + 1)
                part = out_sb[:, m, c * QC:(c + 1) * QC]
                dve.tensor_tensor(part, sum_ps[m][:, :], part, ALU.add).then_inc(sum_done[m], 1)

            def step(ph, name, *numbers):
                n = [int(x) for x in numbers]
                if name == "lG":
                    low_g(ph, *n)
                elif name == "lW":
                    rest()
                elif name in ("lV", "lXT", "lFD"):
                    dst_h, dst_l = {"lV": (v_h, v_l), "lXT": (xt_h, xt_l), "lFD": (fd_h, fd_l)}[name]
                    low_score(ph, f"{name[1:]}.{n[0]}", dst_l[:, 4 * n[0]:4 * n[0] + 4, :],
                              dst_h[:, 4 * n[0]:4 * n[0] + 4, :])
                elif name in ("max0", "max2"):
                    negmax = negmax0 if name == "max0" else negmax2
                    row_max(ph, f"S{name[3]}.{n[0]}", negmax[:, n[0]:n[0] + 1])
                elif name in ("norm0", "norm2"):
                    normalise(ph, name[4], *n)
                elif name in ("r0", "r2"):
                    reciprocal(ph, name[1], *n)
                elif name in ("lT0", "lT2"):
                    low_turn(ph, name[2], *n)
                elif name == "lFBC":
                    low_fbc(ph)
                elif name == "minE":
                    min_e(ph)
                elif name == "nE":
                    normalise_e(ph)
                elif name == "lET":
                    s = ph.slot(TURN, "ET")
                    dve.wait_ge(turn_staged[s], ph.staged(TURN, "ET") + 1)
                    low(et_l[:, :, :], turn_ps[s][:, :].rearrange("p (m c) -> p m c", c=C), et_h[:, :, :])\
                        .then_inc(turn_done[s], 1)
                elif name == "fx":
                    finish_x1(ph, *n)
                elif name == "fo":
                    finish_out(ph, *n)
                elif name == "bn":
                    bn_stats(ph.i + 1)
                elif name == "spread":
                    spread(ph, ph.i + 1)
                elif name == "gvar":
                    group_var(ph, ph.i + 1)
                elif name == "xn":
                    dve.wait_ge(turn_full[ph.slot(TURN, "T0.7.1")], ph.uses(TURN, "T0.7.1") + 1)
                    make_xn(ph.i + 1, *n)
            phases(dve, DVE_PHASES, step)

        @block.tensor
        def _(pe):
            def product(dst, lhs, rhs, start, stop):
                pe.matmul(dst, lhs[0], rhs[0], start=start, stop=False)
                pe.matmul(dst, lhs[0], rhs[1], start=False, stop=False)
                return pe.matmul(dst, lhs[1], rhs[0], start=False, stop=stop)

            pe.wait_ge(consts_made, 6)

            def group_average(s, n, src, ready, count):
                pe.wait_ge(ready, count)
                if not (isinstance(n, int) and n == 0):
                    pe.wait_ge(turn_done[s], n)
                pe.matmul(turn_ps[s][:, 0:CH * RUNS], group_mean[:, :], src, start=True, stop=True)\
                    .then_inc(turn_full[s], 1)

            def weight_product(ps, lhs, rhs):
                for m in range(CH):
                    for oh in range(CH):
                        last = pe.matmul(ps[:, m * C:(m + 1) * C], lhs[:, oh, m * P:(m + 1) * P], rhs[:, oh, :],
                                         start=(oh == 0), stop=(oh == CH - 1))
                return last

            def bias_product(ps, *terms):
                for m in range(CH):
                    for n, (w, v) in enumerate(terms):
                        for oh in range(CH):
                            last = pe.matmul(ps[:, m:m + 1], w[:, oh, m * P:(m + 1) * P], vecs[:, v, oh:oh + 1],
                                             start=(n == 0 and oh == 0), stop=(n == len(terms) - 1 and oh == CH - 1))
                return last

            def turn_weight(ps, w):
                for m in range(CH):
                    for oh in range(CH):
                        last = pe.transpose(ps[:, m * C + oh * P:m * C + (oh + 1) * P],
                                            w[:, oh, m * P:(m + 1) * P], ident[:, :])
                return last

            group_average(0, 0, bn_parts[:, :, 1], bn_made, CH)
            pe.wait_ge(wo_loaded, 16)
            turn_weight(sum_ps[0], wo_sb).then_inc(wot_turned, 1)
            group_average(1, 0, spread_sb[:, :], turn_done[0], 1)
            pe.wait_ge(wq_loaded, 16)
            pe.wait_ge(wkg_made, 1)
            weight_product(a_ps, wq_sb, wkg_sb).then_inc(a_full, 1)
            pe.wait_ge(wv_loaded, 16)
            pe.wait_ge(wot_made, 1)
            weight_product(b_ps, wv_sb, wot_sb).then_inc(b_full, 1)

            def g_bias():
                pe.wait_ge(g_vecs_loaded, 16 * 2)
                pe.wait_ge(a_copied, 1)
                bias_product(turn_ps[0], (a1_sb, GN_B), (wkg_sb, BQ)).then_inc(g_bias_full, 1)

            def rest():
                pe.wait_ge(block1_loaded, 16 * 3)
                pe.wait_ge(b_copied, 1)
                turn_weight(sum_ps[0], wd_sb)
                for ih in range(CH):
                    for n, w in enumerate((wb_sb, wb_sb, wc_sb)):
                        at = (ih * 3 + n) * C8
                        pe.transpose(sum_ps[1][:, at:at + C8], w[:, ih * P:(ih + 1) * P], ident[0:C8, 0:C8])
                pe.wait_ge(vecs_loaded, 16 * 8)
                bias_product(sum_ps[1][:, C_BIAS_AT:C_BIAS_AT + CH], (b1_sb, GN_B), (wot_sb, BV)).then_inc(rest_full, 1)

            def after(ph, *uses):
                for use in ph.last_uses(SCORE, uses):
                    pe.wait_ge(score_done[ph.slot(SCORE, use)], ph.uses(SCORE, use) + 1)

            def enter(ph, use, *reads):
                s = ph.slot(SCORE, use)
                after(ph, *(r for r in ph.last_uses(SCORE, reads) if ph.slot(SCORE, r) != s))
                wait(pe, score_done[s], ph.uses(SCORE, use))
                return s, score_ps[s]

            def cols(t, n=P):
                return slice(t * n, (t + 1) * n)

            def both(parts, *index):
                return [p[index] for p in parts]

            xn_p, g_p, v_p, x1_p, fd_p = (xn_h, xn_l), (g_h, g_l), (v_h, v_l), (x1_h, x1_l), (fd_h, fd_l)
            pt0_p, pt2_p, xt_p, et_p = (pt0_h, pt0_l), (pt2_h, pt2_l), (xt_h, xt_l), (et_h, et_l)
            every = slice(None)

            def project_g(ph, c):
                if ph.like == 0 and c == 0:
                    pe.wait_ge(x0_low, 1)
                    pe.wait_ge(a_made, 1)
                else:
                    pe.wait_ge(xn_split, ph.i * XN + XN)
                s, ps = enter(ph, f"G.{c}")
                for m in range(CH):
                    if ph.like == 0 and c == 0 and m == 1:
                        pe.wait_ge(a_copied, 1)
                    for k in range(CH):
                        last = product(ps[:, cols(m, QC)], both(a_w, every, k, cols(m)),
                                       both(xn_p, every, k, cols(c, QC)), k == 0, k == CH - 1)
                last.then_inc(score_full[s], 1)

            def project_rows(ph, use, u, data, w):
                s, ps = enter(ph, use)
                for t in range(4):
                    for k in range(CH):
                        last = product(ps[:, cols(t, C)], both(data, every, k, cols(4 * u + t)),
                                       both(w, every, k, every), k == 0, k == CH - 1)
                last.then_inc(score_full[s], 1)

            def scores0(ph, j):
                if ph.like == 0 and j == 0:
                    pe.wait_ge(xn_split, XN)
                s, ps = enter(ph, f"S0.{j}", *([f"G.{j // QT}"] if j % QT == 0 else []))
                for n in range(2):
                    for k in range(CH):
                        last = product(ps[:, cols(n, QC)], both(g_p, every, k, cols(j % QT)),
                                       both(xn_p, every, k, cols(n, QC)), k == 0, k == CH - 1)
                last.then_inc(score_full[s], 1)

            def scores2(ph, j):
                s, ps = enter(ph, f"S2.{j}", *(["FBC"] if j == 0 else []))
                for n in range(2):
                    last = pe.matmul(ps[:, cols(n, QC)], fb_parts[:, cols(j)], fc_parts[:, cols(n, QC)],
                                     start=True, stop=True)
                last.then_inc(score_full[s], 1)

            def enter_turn(ph, use):
                s = ph.slot(TURN, use)
                wait(pe, turn_done[s], ph.uses(TURN, use))
                return s, turn_ps[s]

            def turn(ph, block, j, h):
                made, before = (probs0_made, ph.i) if block == "0" else (probs2_made, ph.i - 1)
                pe.wait_ge(made, before * TILES + (j + 1))
                s, ps = enter_turn(ph, f"T{block}.{j}.{h}")
                rows = probs_of(ph, block, j)
                for t in range(4):
                    last = pe.transpose(ps[:, cols(t)], rows[:, cols(4 * h + t)], ident[:, :])
                last.then_inc(turn_full[s], 1)

            def turn_x1(ph, u):
                if ph.like == 1:
                    for m in range(CH):
                        pe.wait_ge(sum_done[m], CHUNKS)
                s, ps = enter(ph, f"XT.{u}")
                for t in range(4):
                    for k in range(CH):
                        last = pe.transpose(ps[:, t * C + k * P:t * C + (k + 1) * P], x1[:, k, cols(4 * u + t)],
                                            ident[:, :])
                last.then_inc(score_full[s], 1)

            def project_fbc(ph):
                pe.wait_ge(x1_split, ph.i * CH)
                s, ps = enter(ph, "FBC")
                for n in range(2):
                    for k in range(CH):
                        last = product(ps[0:3 * C8, cols(n, QC)], both(bbc_w, every, k, every),
                                       both(x1_p, every, k, cols(n, QC)), k == 0, k == CH - 1)
                last.then_inc(score_full[s], 1)

            def channel_scores(ph):
                s, ps = enter(ph, "ATT", "XT.0", "XT.1")
                for m in range(CH):
                    for t in range(NT):
                        last = product(ps[:, cols(m, C)], both(xt_p, every, t, cols(m)),
                                       both(xt_p, every, t, every), t == 0, t == NT - 1)
                last.then_inc(score_full[s], 1)

            def channel_turn(ph):
                pe.wait_ge(e_made, ph.i * CH)
                s, ps = enter_turn(ph, "ET")
                for dh in range(CH):
                    for m in range(CH):
                        last = pe.transpose(ps[:, dh * C + m * P:dh * C + (m + 1) * P], e_sb[:, m, cols(dh)],
                                            ident[:, :])
                last.then_inc(turn_full[s], 1)

            def turned(ph, uses):
                for use in ph.last_uses(TURN, uses):
                    pe.wait_ge(turn_done[ph.slot(TURN, use)], ph.uses(TURN, use) + 1)

            def sum_steps(ph, block, c):
                v = v_p if block == "0" else fd_p
                pt = turned_of(ph, block, c)
                use = f"O{block}.{c}"
                if block == "2":
                    if c == 0:
                        turned(ph, ["ET"])
                    for m in range(CH):
                        wait(pe, sum_done[m], ph.uses(SUM, use, m))
                        for k in range(CH):
                            last = product(sum_ps[m][:, :], both(et_p, every, k, cols(m)),
                                           both(x1_p, every, k, cols(c, QC)), k == 0, False)
                        if c == CHUNKS - 1 and m == CH - 1:
                            last.then_inc(x1_read, 1)
                        yield
                turned(ph, [f"T{block}.{QT * c + j}.{h}" for j in range(QT) for h in range(2)])
                if c == 0:
                    after(ph, *(["V.0", "V.1"] if block == "0" else ["FD.0", "FD.1"]))
                for half, m in ((half, m) for half in range(2) for m in range(CH)):
                    if block == "0" and half == 0:
                        wait(pe, sum_done[m], ph.uses(SUM, use, m))
                        if ph.like == 0 and c == 0:
                            pe.wait_ge(rest_made, 1)
                    for k in range(half * NT // 2, (half + 1) * NT // 2):
                        last = product(sum_ps[m][:, :], both(v, every, k, cols(m)), both(pt, every, k, every),
                                       block == "0" and k == 0, k == NT - 1)
                        if k == NT - 1:
                            last.then_inc(sum_full[m], 1)
                        yield

            sums = {}

            def sum_on(ph, block, c, steps):
                key = ph.like, block, c
                if key not in sums:
                    sums[key] = sum_steps(ph, block, c)
                for _ in range(steps):
                    next(sums[key])

            def stats(ph, use):
                s = ph.slot(TURN, use)
                if use == "MEAN":
                    group_average(s, ph.uses(TURN, use), bn_parts[:, :, 1], bn_made, ph.i * CH + 2 * CH)
                else:
                    m = ph.slot(TURN, "MEAN")
                    group_average(s, 0 if m == s else ph.uses(TURN, use), spread_sb[:, :], turn_done[m],
                                  ph.uses(TURN, use) if m == s else ph.uses(TURN, "MEAN") + 1)

            def step(ph, name, *numbers):
                if name in ("O0", "O2"):
                    sum_on(ph, name[1], int(numbers[0]), int(numbers[1][1:]))
                    return
                n = [int(x) for x in numbers]
                if name == "G":
                    project_g(ph, *n)
                elif name == "BG":
                    g_bias()
                elif name == "W":
                    rest()
                elif name == "V":
                    if ph.like == 0 and n[0] == 0:
                        pe.wait_ge(b_made, 1)
                        pe.wait_ge(b_copied, 1)
                    else:
                        pe.wait_ge(xn_split, ph.i * XN + XN)
                    project_rows(ph, f"V.{n[0]}", n[0], xn_p, b_w)
                elif name == "FD":
                    pe.wait_ge(x1_split, ph.i * CH)
                    project_rows(ph, f"FD.{n[0]}", n[0], x1_p, d_w)
                elif name == "S0":
                    scores0(ph, *n)
                elif name == "S2":
                    scores2(ph, *n)
                elif name in ("T0", "T2"):
                    turn(ph, name[1], *n)
                elif name == "XT":
                    turn_x1(ph, *n)
                elif name == "FBC":
                    project_fbc(ph)
                elif name == "ATT":
                    channel_scores(ph)
                elif name == "ET":
                    channel_turn(ph)
                elif name in STATS:
                    stats(ph, name)
            phases(pe, PE_PHASES, step)


_INS = ["x"] + [f"L0_conv_{n}" for n in ("gn_w", "gn_b", "wq", "bq", "wk", "bk", "wv", "bv", "wo", "bo")] \
    + [f"L1_conv_{n}" for n in ("wb", "bb", "wc", "bc", "wd", "bd", "alpha", "beta")]
_OUTS = [((BATCH, C, 32, 32), "float32")]


def kernel(**inputs):
    import numpy as _np
    import concourse.bacc as _bacc
    from concourse import mybir as _mybir
    from concourse.bass_utils import run_bass_kernel_spmd as _run

    nc = _bacc.Bacc("TRN2", target_bir_lowering=False, num_devices=1)
    arrays, args = {}, []
    for name in _INS:
        a = _np.ascontiguousarray(inputs[name])
        arrays[f"in_{name}_dram"] = a
        args.append(nc.dram_tensor(f"in_{name}_dram", a.shape, _mybir.dt.from_np(a.dtype), kind="ExternalInput").ap())
    for i, (shape, dtype) in enumerate(_OUTS):
        dt = _mybir.dt.from_np(_np.dtype(dtype))
        args.append(nc.dram_tensor(f"out_{i}_dram", shape, dt, kind="ExternalOutput").ap())
    dual_attention_kernel(nc, *args)
    r = _run(nc, [arrays], core_ids=[0])
    return r.results[0]["out_0_dram"]
```

```python
import concourse.bass as bass
from concourse import mybir
from contextlib import ExitStack

BATCH, C, N = 4, 256, 1024
C8, GROUPS = 32, 32
EPS = 1e-5
P = 128
CH = C // P
QC = 512
CHUNKS = N // QC
QT = QC // P
NT = N // P
TILES = CHUNKS * QT

PE_FIRST = """
    G.0 BG W V.0 S0.0 S0.1 S0.2 T0.0.0 T0.0.1 S0.3 T0.1.0 T0.1.1 G.1 V.1 MEAN T0.2.0 VAR T0.2.1 T0.3.0 S0.4
    T0.3.1 S0.5 S0.6 T0.4.0 O0.0x1 T0.4.1 S0.7 O0.0x1 T0.5.0 T0.5.1 O0.0x3 T0.6.0 O0.0x4 T0.6.1 T0.7.0 O0.0x4
    T0.7.1 O0.0x3 O0.1x16 NG NV
""".split()
PE_STEADY = """
    XT.0 XT.1 S0.0 S0.1 S0.2 T0.0.0 T0.0.1 S0.3 T0.1.0 G.1 T0.1.1 V.1 T0.2.0 T0.2.1 S0.4 T0.3.0 T0.3.1 FBC ATT
    O0.0x3 AT S2.0 O0.0x1 S2.1 O0.0x3 FD.0 T2.0.0 T2.0.1 S2.2 O0.0x3 T2.1.0 O0.0x1 T2.1.1 O0.0x1 FD.1 O0.0x1
    S2.3 O0.0x2 ET MEAN S0.5 VAR T2.2.0 O0.0x1 T2.2.1 S0.6 T2.3.0 S2.4 O2.0x1 T2.3.1 O2.0x1 T0.4.0 O2.0x1
    T0.4.1 O2.0x1 S2.5 O2.0x1 T0.5.0 S0.7 T0.5.1 O2.0x6 T0.6.0 O2.0x1 T0.6.1 O2.0x1 T0.7.0 O2.0x2 T0.7.1
    O2.0x3 T2.4.0 O0.1x1 T2.4.1 S2.6 O0.1x1 T2.5.0 O0.1x3 T2.5.1 S2.7 O0.1x4 T2.6.0 O0.1x5 T2.6.1 O0.1x2
    T2.7.0 T2.7.1 O2.1x7 NV O2.1x3 NG O2.1x8
""".split()
PE_LAST = """
    XT.0 p:O2.1x2 XT.1 FBC p:O2.1x2 ATT p:O2.1x1 AT p:O2.1x1 S2.0 p:O2.1x1 S2.1 S2.2 ET p:O2.1x1 S2.3 T2.0.0
    T2.0.1 FD.0 T2.1.0 T2.1.1 FD.1 T2.2.0 T2.2.1 S2.4 T2.3.0 O2.0x1 T2.3.1 O2.0x1 S2.5 S2.6 O2.0x1 T2.4.0
    O2.0x1 T2.4.1 O2.0x2 S2.7 O2.0x4 T2.5.0 T2.5.1 O2.0x2 T2.6.0 T2.6.1 O2.0x4 T2.7.0 O2.0x2 T2.7.1 O2.1x18
""".split()
ACT_FIRST = """
    hG.0 hV.0 xcopyI hW exp0.0 exp0.1 hT0.0.0 hT0.0.1 exp0.2 hT0.1.0 hT0.1.1 exp0.3 hG.1 hT0.2.0 hT0.2.1
    hT0.3.0 hV.1 hT0.3.1 exp0.4 exp0.5 hT0.4.0 hT0.4.1 exp0.6 hT0.5.0 hT0.5.1 exp0.7 hT0.6.0 hT0.6.1 hT0.7.0
    hT0.7.1 xnh.0 xnh.1 x1h.0 hNG x1h.1 hNV
""".split()
ACT_STEADY = """
    hXT.0 hXT.1 exp0.0 exp0.1 hT0.0.0 hT0.0.1 exp0.2 exp0.3 hT0.1.0 hT0.1.1 hG.1 hT0.2.0 hT0.2.1 hV.1 hT0.3.0
    exp0.4 hT0.3.1 hFBC cA base.0 base.1 xcopyI exp2.0 exp2.1 expE hT2.0.0 hT2.0.1 hFD.0 hT2.1.0 exp2.2
    hT2.1.1 hFD.1 hET exp2.3 hT2.2.0 exp0.5 hT2.2.1 hT2.3.0 hT2.3.1 exp0.6 hT0.4.0 exp2.4 hT0.4.1 hT0.5.0
    hT0.5.1 exp0.7 hT0.6.0 hT0.6.1 exp2.5 hT0.7.0 hT0.7.1 hT2.4.0 hT2.4.1 exp2.6 hT2.5.0 hT2.5.1 xnh.0 exp2.7
    xnh.1 hT2.6.0 hT2.6.1 hT2.7.0 hT2.7.1 x1h.0 hNV hNG x1h.1
""".split()
ACT_LAST = """
    hXT.0 hXT.1 hFBC cA expE exp2.0 exp2.1 hET exp2.2 hT2.0.0 hT2.0.1 exp2.3 hT2.1.0 hT2.1.1 hFD.0 hT2.2.0
    hT2.2.1 hFD.1 hT2.3.0 exp2.4 hT2.3.1 exp2.5 hT2.4.0 hT2.4.1 exp2.6 base.0 base.1 hT2.5.0 hT2.5.1 hT2.6.0
    exp2.7 hT2.6.1 hT2.7.0 hT2.7.1
""".split()
DVE_FIRST = """
    lG.0 lV.0 max0.0 lW norm0.0 max0.1 max0.2 norm0.1 lT0.0.0 lT0.0.1 norm0.2 max0.3 lT0.1.0 bn lT0.1.1
    norm0.3 spread lT0.2.0 gvar lG.1 lT0.2.1 lV.1 max0.4 lT0.3.0 norm0.4 max0.5 lT0.3.1 norm0.5 max0.6 lT0.4.0
    lT0.4.1 norm0.6 lT0.5.0 max0.7 lT0.5.1 norm0.7 lT0.6.0 lT0.6.1 lT0.7.0 fx.0.0 xn.0 lT0.7.1 fx.0.1 xn.1
    fx.1.0 fx.1.1 lNG lNV
""".split()
DVE_STEADY = """
    lXT.0 lXT.1 max0.0 max0.1 norm0.0 norm0.1 max0.2 lT0.0.0 lT0.0.1 norm0.2 max0.3 lT0.1.0 lT0.1.1 lG.1
    norm0.3 lT0.2.0 lT0.2.1 lV.1 max0.4 lT0.3.0 lT0.3.1 lFBC sA max2.0 max2.1 aA norm2.0 minE norm2.1 lT2.0.0
    nE lT2.0.1 lFD.0 lT2.1.0 max2.2 bn lT2.1.1 lFD.1 norm2.2 spread lET max2.3 gvar max0.5 norm2.3 lT2.2.0
    fx.0.0 lT2.2.1 max0.6 fx.0.1 norm0.4 lT2.3.0 lT2.3.1 norm0.5 max2.4 lT0.4.0 lT0.4.1 norm0.6 lT0.5.0 max0.7
    max2.5 lT0.5.1 norm0.7 lT0.6.0 lT0.6.1 norm2.4 lT0.7.0 lT0.7.1 fo.0.0 norm2.5 fo.0.1 lT2.4.0 lT2.4.1
    max2.6 xn.0 lT2.5.0 xn.1 norm2.6 max2.7 lT2.5.1 fx.1.0 norm2.7 lT2.6.0 lT2.6.1 fx.1.1 lT2.7.0 lT2.7.1 lNV
    lNG fo.1.0 fo.1.1
""".split()
DVE_LAST = """
    lXT.0 lXT.1 p:fo.1.0 lFBC sA aA minE max2.0 max2.1 nE max2.2 norm2.0 lET norm2.1 max2.3 lT2.0.0 lT2.0.1
    norm2.2 norm2.3 lT2.1.0 lT2.1.1 lFD.0 p:fo.1.1 lT2.2.0 max2.4 lT2.2.1 lFD.1 lT2.3.0 lT2.3.1 norm2.4 max2.5
    max2.6 norm2.5 max2.7 lT2.4.0 lT2.4.1 norm2.6 lT2.5.0 lT2.5.1 lT2.6.0 norm2.7 fo.0.0 lT2.6.1 fo.0.1
    lT2.7.0 lT2.7.1 fo.1.0 fo.1.1
""".split()
POOL_FIRST = """
    loadI rstd xnl.0 xnl.1 x1l.0 x1l.1
""".split()
POOL_STEADY = """
    loadI rstd xnl.0 xnl.1 stI.0.0 x1l.0 stI.0.1 stI.1.0 stI.1.1 st.1 x1l.1
""".split()
POOL_LAST = """
    p:stI.1.0 p:stI.1.1 p:st.1
""".split()
NEXT_BATCH = {"NG", "NV", "hNG", "hNV", "lNG", "lNV",
              "loadI", "bn", "MEAN", "spread", "VAR", "gvar", "rstd", "xn", "xnh", "xnl"}
STATS = ["MEAN", "VAR"]
CARRIED = 8
C_BIAS_AT = 256
SCORE_KINDS = {"G", "V", "NG", "NV", "S0", "XT", "FBC", "FD", "ATT", "S2"}
TURN_KINDS = {"AT", "T0", "T2", "ET", "MEAN", "VAR"}


def kind(step):
    return step.split(".")[0]


def without_next(steps):
    return [s for s in steps if kind(s) not in NEXT_BATCH]


def without_carried(steps):
    steps, left = [s for s in steps if s not in ("fo.1.0", "fo.1.1", "stI.1.0", "stI.1.1", "st.1")], CARRIED
    for n in range(len(steps) - 1, -1, -1):
        if steps[n].startswith("O2.1x") and left:
            here = int(steps[n][len("O2.1x"):])
            steps[n] = f"O2.1x{max(here - left, 0)}"
            left = max(left - here, 0)
    return [s for s in steps if s != "O2.1x0"]


def per_phase(first, steady, last):
    return [first, steady, steady, without_carried(without_next(steady)), last]


def uses_of(kinds, steps):
    return [s for s in steps if kind(s) in kinds]


def sums_of(steps):
    return list(dict.fromkeys(s.split("x")[0] for s in steps if s[0] == "O"))


class Ring:

    def __init__(self, phases, paired, unstaged=()):
        self.at = []
        self.paired = paired
        used, staged = [0, 0], [0, 0]
        self.start = []
        for names in phases:
            self.start.append((tuple(used), tuple(staged)))
            table = {}
            for n, name in enumerate(names):
                for s in ((0, 1) if paired else (n % 2,)):
                    table[name, s if paired else None] = (s, used[s], staged[s])
                    used[s] += 1
                    staged[s] += name not in unstaged
            self.at.append(table)


class Phase:

    def __init__(self, i, like):
        self.i, self.like = i, like
        self.fixed = isinstance(i, int)
        self.zero, self.one = like < BATCH, like > 0

    def count(self, n_like, per_phase):
        if self.fixed:
            return n_like
        return self.i * per_phase + (n_like - self.like * per_phase)

    def slot(self, ring, use, half=None):
        return ring.at[self.like][use, half][0]

    def _nth(self, ring, use, half, what):
        s = self.slot(ring, use, half)
        n = ring.at[self.like][use, half][1 + what]
        a, b = ring.start[LOOP[0]][what][s], ring.start[LOOP[0] + 1][what][s]
        return self.count(n, b - a)

    def uses(self, ring, use, half=None):
        return self._nth(ring, use, half, 0)

    def staged(self, ring, use, half=None):
        return self._nth(ring, use, half, 1)

    def last_uses(self, ring, uses):
        at = ring.at[self.like]
        return {at[u, None][0]: u for u in sorted(uses, key=lambda u: at[u, None][1])}.values()


LOOP = (1, 3)
PE_PHASES = per_phase(PE_FIRST, PE_STEADY, PE_LAST)
ACT_PHASES = per_phase(ACT_FIRST, ACT_STEADY, ACT_LAST)
DVE_PHASES = per_phase(DVE_FIRST, DVE_STEADY, DVE_LAST)
POOL_PHASES = per_phase(POOL_FIRST, POOL_STEADY, POOL_LAST)
SCORE = Ring([uses_of(SCORE_KINDS, steps) for steps in PE_PHASES], False)
TURN = Ring([STATS + uses_of(TURN_KINDS, PE_PHASES[0])] + [uses_of(TURN_KINDS, steps) for steps in PE_PHASES[1:]],
            False, unstaged=STATS + ["AT"])
SUM = Ring([sums_of(steps) for steps in PE_PHASES], True)


def dual_attention_kernel(nc, x, gn_w, gn_b, wq, bq, wk, bk, wv, bv, wo, bo,
                          wb, bb, wc, bc, wd, bd, alpha, beta, out):
    f32, f32r = mybir.dt.float32, mybir.dt.float32r
    ALU = mybir.AluOpType
    ACT = mybir.ActivationFunctionType
    AX = mybir.AxisListType

    x_dram = x.rearrange("b (m p) h w -> b p m (h w)", p=P)
    out_dram = out.rearrange("b (m p) h w -> b p m (h w)", p=P)

    ctx = ExitStack()
    with ctx:
        def sb(name, shape, dt=f32):
            return ctx.enter_context(nc.sbuf_tensor(name, shape, dt))

        def sem(name):
            return ctx.enter_context(nc.semaphore(name))

        def pair(name):
            return [sem(f"{name}_{s}") for s in range(2)]

        a_w = [sb(f"a_w_{p}", [P, CH, C], f32r) for p in "hl"]
        b_w = [sb(f"b_w_{p}", [P, CH, C], f32r) for p in "hl"]
        d_w = [sb(f"d_w_{p}", [P, CH, C], f32r) for p in "hl"]
        bbc_w = [sb(f"bbc_w_{p}", [P, CH, 3 * C8], f32r) for p in "hl"]
        ident = sb("ident", [P, P])
        group_mean = sb("group_mean", [P, P])
        GN_W, GN_B, BQ, BV, BO, BD, G_BIAS, C_BIAS, ALPHA_BD = range(9)
        vecs = sb("vecs", [P, 9, CH])
        bbc_bias = sb("bbc_bias", [3 * C8, 1])
        gains = sb("gains", [P, 2])

        x_in = sb("x_in", [P, CH, N])
        x1 = sb("x1", [P, CH, N])
        xn_h = sb("xn_h", [P, CH, N], f32r)
        xn_l = sb("xn_l", [P, CH, N], f32r)
        g_h = sb("g_h", [P, CH, QC], f32r)
        g_l = sb("g_l", [P, CH, QC], f32r)
        v_h = sb("v_h", [P, NT, C], f32r)
        v_l = sb("v_l", [P, NT, C], f32r)
        probs0 = sb("probs0", [P, 3, N])
        probs2 = sb("probs2", [P, 2, N])
        pt0_h = sb("pt0_h", [P, NT, QC], f32r)
        pt0_l = sb("pt0_l", [P, NT, QC], f32r)
        pt2_h = sb("pt2_h", [P, NT, QC], f32r)
        pt2_l = sb("pt2_l", [P, NT, QC], f32r)
        x1_h = sb("x1_h", [P, CH, N], f32r)
        x1_l = sb("x1_l", [P, CH, N], f32r)
        fd_h = sb("fd_h", [P, NT, C], f32r)
        fd_l = sb("fd_l", [P, NT, C], f32r)
        fb_parts = sb("fb_parts", [3 * C8, N], f32r)
        fc_parts = sb("fc_parts", [3 * C8, N], f32r)
        et_h = sb("et_h", [P, CH, C], f32r)
        et_l = sb("et_l", [P, CH, C], f32r)
        out_sb = sb("out_sb", [P, CH, N])
        RUNS = 4
        bn_raw = sb("bn_raw", [P, CH, 2, 6])
        bn_parts = bn_raw[:, :, :, :].rearrange("p m h (e t) -> p (m h e) t", t=3)
        diff, square = sb("diff", [P, CH, RUNS]), sb("square", [P, CH, RUNS])
        spread_sb = sb("spread_sb", [P, CH * RUNS])
        stat = sb("stat", [P, 4, CH])
        GMEAN, VARIANCE, GVAR, RSTD = range(4)
        power = sb("power", [P, CH])
        negmax0, rowsum0, recip0 = (sb(f"{n}0", [P, TILES]) for n in ("negmax", "rowsum", "recip"))
        negmax2, rowsum2, recip2 = (sb(f"{n}2", [P, TILES]) for n in ("negmax", "rowsum", "recip"))
        rowmin_e, rowsum_e, recip_e = (sb(f"{n}_e", [P, CH]) for n in ("rowmin", "rowsum", "recip"))

        xt_h = pt2_h[:, 0:NT // 2, :].rearrange("p a (b c) -> p (a b) c", c=C)
        xt_l = pt2_l[:, 0:NT // 2, :].rearrange("p a (b c) -> p (a b) c", c=C)
        xn = probs0[:, 0:CH, :]
        e_sb = probs0[:, 2, 0:CH * C].rearrange("p (m d) -> p m d", d=C)
        cross_sb = probs0[:, 2, CH * C:2 * CH * C].rearrange("p (m d) -> p m d", d=C)
        out_flat = out_sb[:, :, :].rearrange("p m n -> p (m n)")

        def in_w(n):
            return out_flat[:, n * CH * C:(n + 1) * CH * C].rearrange("p (m c) -> p m c", c=C)
        wq_sb, wk_sb, wv_sb, wo_sb = (in_w(n) for n in range(4))
        p2_flat = probs2[:, :, :].rearrange("p s n -> p (s n)")
        wd_sb = p2_flat[:, 0:CH * C].rearrange("p (m c) -> p m c", c=C)
        wkg_sb = p2_flat[:, CH * C:2 * CH * C].rearrange("p (m c) -> p m c", c=C)
        wb_sb = p2_flat[0:C8, 2 * CH * C:2 * CH * C + C]
        wc_sb = p2_flat[0:C8, 2 * CH * C + C:2 * CH * C + 2 * C]
        gw_row = p2_flat[:, 2 * CH * C + 2 * C:2 * CH * C + 3 * C]
        x1_flat = x1[:, :, :].rearrange("p m n -> p (m n)")
        wot_sb, a1_sb, b1_sb = (x1_flat[:, n * CH * C:(n + 1) * CH * C].rearrange("p (m c) -> p m c", c=C)
                                for n in range(3))

        def probs_of(ph, block, j):
            if block == "0":
                ring = [probs0[:, n, :] for n in range(3)] + ([] if ph.one else [probs2[:, 0, :]])
            else:
                ring = [probs2[:, n, :] for n in range(2)] + ([] if ph.zero else [probs0[:, n, :] for n in range(2)])
            return ring[j % len(ring)]

        def turned_of(ph, block, c):
            other = c == 1 and not (ph.one and ph.zero)
            return (pt0_h, pt0_l) if (block == "0") != other else (pt2_h, pt2_l)

        score_ps = [ctx.enter_context(nc.psum_tensor(f"score_ps_{s}", [P, 2 * QC], f32)) for s in range(2)]
        turn_ps = [ctx.enter_context(nc.psum_tensor(f"turn_ps_{s}", [P, QC], f32)) for s in range(2)]
        sum_ps = [ctx.enter_context(nc.psum_tensor(f"sum_ps_{s}", [P, QC], f32)) for s in range(2)]

        a_ps, b_ps = (ps[:, QC:2 * QC] for ps in score_ps)

        score_full, score_staged, score_done = pair("score_full"), pair("score_staged"), pair("score_done")
        turn_full, turn_staged, turn_done = pair("turn_full"), pair("turn_staged"), pair("turn_done")
        sum_full, sum_done = pair("sum_full"), pair("sum_done")
        x0_loaded = pair("x0_loaded")
        x_loaded = pair("x_loaded")
        wk_loaded = sem("wk_loaded")
        wq_loaded, wo_loaded, wv_loaded = sem("wq_loaded"), sem("wo_loaded"), sem("wv_loaded")
        block1_loaded = sem("block1_loaded")
        gn_w_loaded = sem("gn_w_loaded")
        g_vecs_loaded = sem("g_vecs_loaded")
        vecs_loaded = sem("vecs_loaded")
        out_stored = sem("out_stored")
        last_stored = sem("last_stored")
        out_free = sem("out_free")
        x1_read = sem("x1_read")
        consts_made = sem("consts_made")
        xn_made = sem("xn_made")
        xn_high = sem("xn_high")
        xn_split = sem("xn_split")
        x_copied = sem("x_copied")
        probs0_made = sem("probs0_made")
        probs2_made = sem("probs2_made")
        rowmin_made = sem("rowmin_made")
        exp_e_made = sem("exp_e_made")
        e_made = sem("e_made")
        x1_high = sem("x1_high")
        x1_split = sem("x1_split")
        base_made = sem("base_made")
        recip_made0, recip_made2, recip_made_e = sem("recip_made0"), sem("recip_made2"), sem("recip_made_e")
        bn_made = sem("bn_made")
        rstd_made = sem("rstd_made")
        dve_step = sem("dve_step")
        wot_turned, wot_made = sem("wot_turned"), sem("wot_made")
        wkg_made = sem("wkg_made")
        a_full, a_high, a_copied, a_made = (sem(f"a_{n}") for n in ("full", "high", "copied", "made"))
        b_full, b_high, b_copied, b_made = (sem(f"b_{n}") for n in ("full", "high", "copied", "made"))
        g_bias_full, g_bias_made = sem("g_bias_full"), sem("g_bias_made")
        rest_full, rest_high, rest_made = sem("rest_full"), sem("rest_high"), sem("rest_made")
        x0_low = sem("x0_low")

        XN = CH * CHUNKS
        BN_STEPS = 4

        block = ctx.enter_context(nc.Block())

        def phases(eng, steps, run_step):
            def body(ph):
                for step in steps[ph.like]:
                    at = ph
                    if step.startswith("p:"):
                        at, step = Phase(ph.i - 1, ph.like - 1), step[2:]
                    name, *numbers = step.replace("x", ".x").split(".") if step[0] == "O" else step.split(".")
                    run_step(at, name, *numbers)
            body(Phase(0, 0))
            with eng.Fori(LOOP[0], LOOP[1]) as i:
                body(Phase(i, LOOP[0]))
            body(Phase(BATCH - 1, BATCH - 1))
            body(Phase(BATCH, BATCH))

        def rows_of(flat):
            return flat.rearrange("p (m c) -> p m c", c=C)

        def wait(eng, semaphore, count):
            if not (isinstance(count, int) and count == 0):
                eng.wait_ge(semaphore, count)

        @block.sync
        def _(sp):
            def load_w(dst, src, semaphore):
                sp.dma_start(dst, src.rearrange("(m p) c -> p m c", p=P)).then_inc(semaphore, 16)

            def load_v(n, v, semaphore):
                with nc.allow_non_contiguous_dma(reason="vectors of 256 words"):
                    sp.dma_start(vecs[:, n, :], v.rearrange("(m p) -> p m", p=P)).then_inc(semaphore, 16)

            for m in range(CH):
                sp.dma_start(x_in[:, m, :], x_dram[0, :, m, :]).then_inc(x0_loaded[m], 16)
            load_w(wo_sb, wo, wo_loaded)
            load_w(wv_sb, wv, wv_loaded)
            load_v(GN_B, gn_b, g_vecs_loaded)
            load_v(BQ, bq, g_vecs_loaded)
            load_w(wd_sb, wd, block1_loaded)
            sp.dma_start(wb_sb, wb).then_inc(block1_loaded, 16)
            sp.dma_start(wc_sb, wc).then_inc(block1_loaded, 16)
            for n, v in ((BV, bv), (BO, bo), (BD, bd)):
                load_v(n, v, vecs_loaded)
            for n, v in enumerate((bb, bb, bc)):
                sp.dma_start(bbc_bias[n * C8:(n + 1) * C8, :], v.rearrange("(p a) -> p a", a=1))\
                    .then_inc(vecs_loaded, 16)
            for n, v in enumerate((alpha, beta)):
                sp.dma_start(gains[:, n:n + 1], v.rearrange("(a c) -> a c", a=1).broadcast_to([P, 1]))\
                    .then_inc(vecs_loaded, 16)

            last = Phase(BATCH, BATCH)
            for c in range(CHUNKS):
                part = slice(c * QC, (c + 1) * QC)
                for m in range(CH):
                    sp.wait_ge(sum_done[m], last.uses(SUM, f"O2.{c}", m) + 1)
                    sp.dma_start(out_dram[BATCH - 1, :, m, part], out_sb[:, m, part]).then_inc(last_stored, 16)
            sp.wait_ge(last_stored, 16 * CHUNKS * CH)

        @block.gpsimd
        def _(pool):
            pool.memset(ident[:, :], 0.0).then_inc(consts_made, 1)
            pool.memset(group_mean[:, :], float(GROUPS) / C / RUNS).then_inc(consts_made, 1)
            pool.memset(power[:, :], -0.5).then_inc(consts_made, 1)
            pool.wait_ge(consts_made, 3)
            pool.affine_select(out=ident[:, :], in_=ident[:, :], compare_op=ALU.not_equal, fill=1.0, base=0,
                               pattern=[[-1, P]], channel_multiplier=1).then_inc(consts_made, 1)
            per = C // GROUPS
            blocks = group_mean[:, :].rearrange("p (g c) -> p g c", c=per)
            pool.affine_select(out=blocks, in_=blocks, compare_op=ALU.is_ge, fill=0.0, base=0,
                               pattern=[[-per, P // per], [0, per]], channel_multiplier=1).then_inc(consts_made, 1)
            pool.wait_ge(consts_made, 5)
            pool.affine_select(out=blocks, in_=blocks, compare_op=ALU.is_ge, fill=0.0, base=per - 1,
                               pattern=[[per, P // per], [0, per]], channel_multiplier=-1).then_inc(consts_made, 1)

            def rstd(s, n):
                pool.wait_ge(turn_done[s], n + 1)
                pool.tensor_tensor(stat[:, RSTD, :], stat[:, GVAR, :], power[:, :], ALU.pow)\
                    .then_inc(rstd_made, 1)

            def split_xn(b, m):
                pool.wait_ge(xn_high, b * XN + (m + 1) * CHUNKS)
                pool.tensor_tensor(xn_l[:, m, :], xn[:, m, :], xn_h[:, m, :].bitcast(f32), ALU.subtract)\
                    .then_inc(xn_split, CHUNKS)

            def split_x1(ph, m):
                pool.wait_ge(x1_high, ph.i * CH + (m + 1))
                pool.tensor_tensor(x1_l[:, m, :], x1[:, m, :], x1_h[:, m, :].bitcast(f32), ALU.subtract)\
                    .then_inc(x1_split, 1)

            def load(ph):
                b = ph.i + 1
                pool.wait_ge(xn_made, ph.i * XN + XN)
                pool.wait_ge(x_copied, ph.i * (CH * 16) + CH * 16)
                src = x_dram[b] if ph.fixed else x_dram[bass.ds(b, 1)][0]
                for m in range(CH):
                    pool.dma_start(x_in[:, m, :], src[:, m, :])\
                        .then_inc(x_loaded[m], 16)

            def store(ph, c, m):
                a = ph.i - 1
                dst = out_dram[a] if ph.fixed else out_dram[bass.ds(a, 1)][0]
                pool.wait_ge(sum_done[m], ph.uses(SUM, f"O2.{c}", m) + 1)
                pool.dma_start(dst[:, m, c * QC:(c + 1) * QC], out_sb[:, m, c * QC:(c + 1) * QC])\
                    .then_inc(out_stored, 16)

            rstd(STATS.index("VAR"), 0)
            late = slice(QC, N)
            for m in range(CH):
                pool.wait_ge(xn_high, CH + (m + 1))
                pool.tensor_tensor(xn_l[:, m, late], xn[:, m, late], xn_h[:, m, late].bitcast(f32), ALU.subtract)\
                    .then_inc(xn_split, CHUNKS)
            pool.sem_inc(out_free, 1)

            def step(ph, name, *numbers):
                n = [int(x) for x in numbers]
                if name == "loadI":
                    load(ph)
                elif name == "stI":
                    store(ph, *n)
                elif name == "st":
                    pool.wait_ge(out_stored, ph.i * (16 * CHUNKS * CH))
                    pool.sem_inc(out_free, 1)
                elif name == "rstd":
                    rstd(ph.slot(TURN, "VAR"), ph.uses(TURN, "VAR"))
                elif name == "xnl":
                    split_xn(ph.i + 1, *n)
                elif name == "x1l":
                    split_x1(ph, *n)
            phases(pool, POOL_PHASES, step)

        @block.scalar
        def _(act):
            act.dma_start(wk_sb, wk.rearrange("(m p) c -> p m c", p=P)).then_inc(wk_loaded, 16)
            act.dma_start(gw_row, gn_w.rearrange("(a c) -> a c", a=1).broadcast_to([P, C])).then_inc(wk_loaded, 16)
            act.dma_start(wq_sb, wq.rearrange("(m p) c -> p m c", p=P)).then_inc(wq_loaded, 16)
            with nc.allow_non_contiguous_dma(reason="a vector of 256 words"):
                act.dma_start(vecs[:, GN_W, :], gn_w.rearrange("(m p) -> p m", p=P)).then_inc(gn_w_loaded, 16)

            def high(dst, src, bias=0.0):
                if isinstance(bias, float):
                    return act.activation(dst, src, ACT.Copy)
                return act.activation(dst, src, ACT.Identity, bias=bias)

            def split_xn(b, m):
                act.wait_ge(xn_made, b * XN + (m + 1) * CHUNKS)
                high(xn_h[:, m, :], xn[:, m, :]).then_inc(xn_high, CHUNKS)

            act.wait_ge(wot_turned, 1)
            act.activation(wot_sb, rows_of(sum_ps[0][:, :]), ACT.Copy).then_inc(wot_made, 1)
            for n, (c, m) in enumerate((c, m) for c in range(CHUNKS) for m in range(CH)):
                part = slice(c * QC, (c + 1) * QC)
                act.wait_ge(xn_made, n + 1)
                high(xn_h[:, m, part], xn[:, m, part]).then_inc(xn_high, 1)
            act.wait_ge(gn_w_loaded, 16)
            for ps, w, full, staged in ((a_ps, a_w, a_full, a_high), (b_ps, b_w, b_full, b_high)):
                act.wait_ge(full, 1)
                for m in range(CH):
                    last = act.activation(w[0][:, m, :], ps[:, m * C:(m + 1) * C], ACT.Copy,
                                          scale=vecs[:, GN_W, m:m + 1])
                last.then_inc(staged, 1)
            for ps, plain, made, copied in ((a_ps, a1_sb, a_made, a_copied), (b_ps, b1_sb, b_made, b_copied)):
                act.wait_ge(made, 1)
                act.activation(plain, rows_of(ps), ACT.Copy).then_inc(copied, 1)

            def rest():
                act.wait_ge(vecs_loaded, 16 * 8)
                act.wait_ge(rest_full, 1)
                act.activation(d_w[0][:, :, :], rows_of(sum_ps[0][:, :]), ACT.Copy, scale=gains[:, 0:1])
                high(bbc_w[0][:, :, :], sum_ps[1][:, 0:CH * 3 * C8].rearrange("p (m c) -> p m c", c=3 * C8))\
                    .then_inc(rest_high, 1)

            def stage_score(ph, use, dst, src_of=lambda ps: ps[:, :], bias=0.0):
                s, n = ph.slot(SCORE, use), ph.uses(SCORE, use)
                act.wait_ge(score_full[s], n + 1)
                high(dst, src_of(score_ps[s]), bias).then_inc(score_staged[s], 1)

            def exp_score(ph, use, dst, neg, total):
                s = ph.slot(SCORE, use)
                act.wait_ge(score_staged[s], ph.staged(SCORE, use) + 1)
                act.activation(dst, score_ps[s][:, :], ACT.Exp, bias=neg, scale=1.0, accum_out=total)\
                    .then_inc(score_done[s], 1)

            def stage_turn(ph, block, j, h):
                use = f"T{block}.{j}.{h}"
                s = ph.slot(TURN, use)
                pt, jj = turned_of(ph, block, j // QT)[0], j % QT
                act.wait_ge(turn_full[s], ph.uses(TURN, use) + 1)
                high(pt[:, h * 4:(h + 1) * 4, jj * P:(jj + 1) * P],
                     turn_ps[s][:, :].rearrange("p (k q) -> p k q", q=P)).then_inc(turn_staged[s], 1)

            def g_high(ph, use):
                s, n = ph.slot(SCORE, use), ph.uses(SCORE, use)
                act.wait_ge(score_full[s], n + 1)
                if use == "G.0":
                    act.wait_ge(g_bias_made, 1)
                for m in range(CH):
                    last = high(g_h[:, m, :], score_ps[s][:, m * QC:(m + 1) * QC], vecs[:, G_BIAS, m:m + 1])
                last.then_inc(score_staged[s], 1)

            def copy_x(ph):
                if ph.one:
                    for use in ph.last_uses(SCORE, ["XT.0", "XT.1"]):
                        act.wait_ge(score_full[ph.slot(SCORE, use)], ph.uses(SCORE, use) + 1)
                    act.wait_ge(x1_split, ph.i * CH)
                    act.wait_ge(base_made, ph.i * CH)
                else:
                    for m in range(CH):
                        act.wait_ge(x0_loaded[m], 16)
                    act.wait_ge(rest_full, 1)
                for m in range(CH):
                    act.dma_start(x1[:, m, :], x_in[:, m, :]).then_inc(x_copied, 16)

            def copy_cross(ph):
                s = ph.slot(SCORE, "ATT")
                act.wait_ge(score_full[s], ph.uses(SCORE, "ATT") + 1)
                act.activation(cross_sb, rows_of(score_ps[s][:, QC:2 * QC]), ACT.Copy).then_inc(score_staged[s], 1)

            def exp_e(ph):
                act.wait_ge(rowmin_made, ph.i)
                for m in range(CH):
                    last = act.activation(e_sb[:, m, :], e_sb[:, m, :], ACT.Exp,
                                          bias=rowmin_e[:, m:m + 1], scale=-1.0, accum_out=rowsum_e[:, m:m + 1])
                last.then_inc(exp_e_made, 1)

            def fbc_high(ph):
                s = ph.slot(SCORE, "FBC")
                act.wait_ge(score_full[s], ph.uses(SCORE, "FBC") + 1)
                high(fb_parts[0:2 * C8, :], score_ps[s][0:2 * C8, :], bbc_bias[0:2 * C8, :])
                high(fc_parts[0:C8, :], score_ps[s][2 * C8:3 * C8, :], bbc_bias[2 * C8:3 * C8, :])
                high(fc_parts[2 * C8:3 * C8, :], score_ps[s][2 * C8:3 * C8, :], bbc_bias[2 * C8:3 * C8, :])\
                    .then_inc(score_staged[s], 1)

            def as_rows(ps):
                return ps[:, :].rearrange("p (t c) -> p t c", c=C)

            def step(ph, name, *numbers):
                n = [int(x) for x in numbers]
                if name == "hG":
                    g_high(ph, f"G.{n[0]}")
                elif name == "hNG":
                    g_high(ph, "NG")
                elif name == "hNV":
                    stage_score(ph, "NV", v_h[:, 0:4, :], as_rows)
                elif name == "hW":
                    rest()
                elif name in ("hV", "hXT", "hFD"):
                    dst = {"hV": v_h, "hXT": xt_h, "hFD": fd_h}[name]
                    stage_score(ph, f"{name[1:]}.{n[0]}", dst[:, 4 * n[0]:4 * n[0] + 4, :], as_rows)
                elif name in ("exp0", "exp2"):
                    j, block = n[0], name[3]
                    neg, total = (negmax0, rowsum0) if block == "0" else (negmax2, rowsum2)
                    exp_score(ph, f"S{block}.{j}", probs_of(ph, block, j), neg[:, j:j + 1], total[:, j:j + 1])
                elif name in ("hT0", "hT2"):
                    stage_turn(ph, name[2], *n)
                elif name == "hFBC":
                    fbc_high(ph)
                elif name == "base":
                    act.wait_ge(out_free, ph.i)
                    act.activation(out_sb[:, n[0], :], x1[:, n[0], :], ACT.Identity, scale=2.0,
                                   bias=vecs[:, ALPHA_BD, n[0]:n[0] + 1]).then_inc(base_made, 1)
                elif name == "xcopyI":
                    copy_x(ph)
                elif name == "cA":
                    copy_cross(ph)
                elif name == "expE":
                    exp_e(ph)
                elif name == "hET":
                    s = ph.slot(TURN, "ET")
                    act.wait_ge(turn_full[s], ph.uses(TURN, "ET") + 1)
                    high(et_h[:, :, :], as_rows(turn_ps[s])).then_inc(turn_staged[s], 1)
                elif name == "xnh":
                    act.wait_ge(score_full[ph.slot(SCORE, "S0.7")], ph.uses(SCORE, "S0.7") + 1)
                    split_xn(ph.i + 1, *n)
                elif name == "x1h":
                    for m in range(CH):
                        act.wait_ge(sum_done[m], ph.uses(SUM, "O0.1", m) + 1)
                    if ph.one:
                        act.wait_ge(x1_read, ph.i)
                    high(x1_h[:, n[0], :], x1[:, n[0], :]).then_inc(x1_high, 1)
            phases(act, ACT_PHASES, step)

        @block.vector
        def _(dve):
            def low(dst, src, high_part, bias=None):
                hp = high_part.bitcast(f32)
                if bias is None:
                    return dve.tensor_tensor(dst, src, hp, ALU.subtract)
                return dve.scalar_tensor_tensor(dst, src, bias, hp, ALU.add, ALU.subtract)

            def link(ins, count):
                ins.then_inc(dve_step, 1)
                dve.wait_ge(dve_step, count)

            def bn_stats(b, later=True):
                for m in range(CH):
                    dve.wait_ge(x_loaded[m] if later else x0_loaded[m], b * 16 if later else 16)
                    for h in range(2):
                        last = dve.bn_stats(out=bn_raw[:, m, h, :], in_=x_in[:, m, h * 512:(h + 1) * 512])
                    last.then_inc(bn_made, 1)

            def spread(ph_or_start, b):
                s, n = stat_use(ph_or_start, "MEAN")
                dve.wait_ge(turn_full[s], n + 1)
                means = bn_parts[:, :, 1].rearrange("p (m r) -> p m r", r=RUNS)
                gmean = stat[:, GMEAN, :]
                link(dve.tensor_reduce(gmean, turn_ps[s][:, 0:CH * RUNS].rearrange("p (m r) -> p m r", r=RUNS),
                                       AX.X, ALU.add), b * BN_STEPS + 1)
                link(dve.tensor_tensor(diff[:, :, :], means, gmean.unsqueeze(2).broadcast_to([P, CH, RUNS]),
                                       ALU.subtract), b * BN_STEPS + 2)
                link(dve.tensor_tensor(square[:, :, :], diff[:, :, :], diff[:, :, :], ALU.mult), b * BN_STEPS + 3)
                dve.scalar_tensor_tensor(spread_sb[:, :], bn_parts[:, :, 2], RUNS / N,
                                         square[:, :, :].rearrange("p m r -> p (m r)"), ALU.mult, ALU.add)\
                    .then_inc(turn_done[s], 1)

            def group_var(ph_or_start, b):
                s, n = stat_use(ph_or_start, "VAR")
                dve.wait_ge(turn_full[s], n + 1)
                link(dve.tensor_reduce(stat[:, VARIANCE, :],
                                       turn_ps[s][:, 0:CH * RUNS].rearrange("p (m r) -> p m r", r=RUNS),
                                       AX.X, ALU.add), b * BN_STEPS + 4)
                dve.tensor_scalar(stat[:, GVAR, :], stat[:, VARIANCE, :], EPS, None, ALU.add)\
                    .then_inc(turn_done[s], 1)

            def normalised(m, part):
                return dve.tensor_scalar(xn[:, m, part], x_in[:, m, part], stat[:, GMEAN, m:m + 1],
                                         stat[:, RSTD, m:m + 1], ALU.subtract, ALU.mult)

            def make_xn(b, m):
                dve.wait_ge(rstd_made, b + 1)
                normalised(m, slice(0, N)).then_inc(xn_made, CHUNKS)

            def stat_use(ph, use):
                if ph is None:
                    return STATS.index(use), 0
                return ph.slot(TURN, use), ph.uses(TURN, use)

            bn_stats(0, later=False)
            dve.wait_ge(wk_loaded, 16 * 2)
            for m in range(CH):
                last = dve.scalar_tensor_tensor(wkg_sb[:, m, :], wk_sb[:, m, :], float(C) ** -0.5, gw_row,
                                                ALU.mult, ALU.mult)
            last.then_inc(wkg_made, 1)
            spread(None, 0)
            group_var(None, 0)
            dve.wait_ge(rstd_made, 1)
            for c in range(CHUNKS):
                for m in range(CH):
                    normalised(m, slice(c * QC, (c + 1) * QC)).then_inc(xn_made, 1)
            for m in range(CH):
                dve.wait_ge(xn_high, m + 1)
                last = low(xn_l[:, m, 0:QC], xn[:, m, 0:QC], xn_h[:, m, 0:QC])
            last.then_inc(x0_low, 1)
            dve.wait_ge(gn_w_loaded, 16)
            for ps, w, staged, made in ((a_ps, a_w, a_high, a_made), (b_ps, b_w, b_high, b_made)):
                dve.wait_ge(staged, 1)
                for m in range(CH):
                    last = dve.scalar_tensor_tensor(w[1][:, m, :], ps[:, m * C:(m + 1) * C],
                                                    vecs[:, GN_W, m:m + 1], w[0][:, m, :].bitcast(f32),
                                                    ALU.mult, ALU.subtract)
                last.then_inc(made, 1)
            dve.wait_ge(g_bias_full, 1)
            dve.tensor_copy(vecs[:, G_BIAS, :], turn_ps[0][:, 0:CH]).then_inc(g_bias_made, 1)

            def rest():
                dve.wait_ge(vecs_loaded, 16 * 8)
                dve.wait_ge(rest_high, 1)
                dve.scalar_tensor_tensor(d_w[1][:, :, :], rows_of(sum_ps[0][:, :]), gains[:, 0:1],
                                         d_w[0][:, :, :].bitcast(f32), ALU.mult, ALU.subtract)
                low(bbc_w[1][:, :, :], sum_ps[1][:, 0:CH * 3 * C8].rearrange("p (m c) -> p m c", c=3 * C8),
                    bbc_w[0][:, :, :])
                dve.tensor_scalar(vecs[:, ALPHA_BD, :], vecs[:, BD, :], gains[:, 0:1], None, ALU.mult)
                dve.tensor_tensor(vecs[:, C_BIAS, :], sum_ps[1][:, C_BIAS_AT:C_BIAS_AT + CH], vecs[:, BO, :], ALU.add)\
                    .then_inc(rest_made, 1)

            def row_max(ph, use, dst):
                s = ph.slot(SCORE, use)
                dve.wait_ge(score_full[s], ph.uses(SCORE, use) + 1)
                dve.tensor_reduce(dst, score_ps[s][:, :], AX.X, ALU.max, negate=True).then_inc(score_staged[s], 1)

            def normalise(ph, block, j):
                use = f"S{block}.{j}"
                s = ph.slot(SCORE, use)
                rowsum, recip, recip_made, made, before = \
                    (rowsum0, recip0, recip_made0, probs0_made, ph.i) if block == "0" else \
                    (rowsum2, recip2, recip_made2, probs2_made, ph.i - 1)
                dve.wait_ge(score_done[s], ph.uses(SCORE, use) + 1)
                dve.reciprocal(recip[:, j:j + 1], rowsum[:, j:j + 1]).then_inc(recip_made, 1)
                dve.wait_ge(recip_made, before * TILES + (j + 1))
                rows = probs_of(ph, block, j)
                dve.tensor_scalar(rows, rows, recip[:, j:j + 1], None, ALU.mult).then_inc(made, 1)

            def low_score(ph, use, dst, high_part):
                s = ph.slot(SCORE, use)
                dve.wait_ge(score_staged[s], ph.staged(SCORE, use) + 1)
                low(dst, score_ps[s][:, :].rearrange("p (t c) -> p t c", c=C), high_part)\
                    .then_inc(score_done[s], 1)

            def low_g(ph, use):
                s = ph.slot(SCORE, use)
                dve.wait_ge(score_staged[s], ph.staged(SCORE, use) + 1)
                for m in range(CH):
                    last = low(g_l[:, m, :], score_ps[s][:, m * QC:(m + 1) * QC], g_h[:, m, :],
                               vecs[:, G_BIAS, m:m + 1])
                last.then_inc(score_done[s], 1)

            def low_turn(ph, block, j, h):
                use = f"T{block}.{j}.{h}"
                s = ph.slot(TURN, use)
                (pt_h, pt_l), jj = turned_of(ph, block, j // QT), j % QT
                dve.wait_ge(turn_staged[s], ph.staged(TURN, use) + 1)
                low(pt_l[:, h * 4:(h + 1) * 4, jj * P:(jj + 1) * P],
                    turn_ps[s][:, :].rearrange("p (k q) -> p k q", q=P),
                    pt_h[:, h * 4:(h + 1) * 4, jj * P:(jj + 1) * P]).then_inc(turn_done[s], 1)

            def low_fbc(ph):
                s = ph.slot(SCORE, "FBC")
                dve.wait_ge(score_staged[s], ph.staged(SCORE, "FBC") + 1)
                low(fb_parts[2 * C8:3 * C8, :], score_ps[s][0:C8, :], fb_parts[0:C8, :], bbc_bias[0:C8, :])
                low(fc_parts[C8:2 * C8, :], score_ps[s][2 * C8:3 * C8, :], fc_parts[2 * C8:3 * C8, :],
                    bbc_bias[2 * C8:3 * C8, :]).then_inc(score_done[s], 1)

            def begin_att(ph):
                s = ph.slot(SCORE, "ATT")
                dve.wait_ge(score_staged[s], ph.staged(SCORE, "ATT") + 1)
                dve.tensor_tensor(e_sb, rows_of(score_ps[s][:, 0:CH * C]), cross_sb, ALU.add)\
                    .then_inc(score_done[s], 1)

            def finish_att(ph):
                s, a = ph.slot(TURN, "AT"), ph.slot(SCORE, "ATT")
                dve.wait_ge(score_done[a], ph.uses(SCORE, "ATT") + 1)
                dve.wait_ge(turn_full[s], ph.uses(TURN, "AT") + 1)
                dve.tensor_tensor(e_sb, rows_of(turn_ps[s][:, :]), e_sb, ALU.add).then_inc(turn_done[s], 1)

            def min_e(ph):
                s = ph.slot(TURN, "AT")
                dve.wait_ge(turn_done[s], ph.uses(TURN, "AT") + 1)
                dve.tensor_reduce(rowmin_e[:, :], e_sb, AX.X, ALU.min).then_inc(rowmin_made, 1)

            def normalise_e(ph):
                dve.wait_ge(exp_e_made, ph.i)
                dve.reciprocal(recip_e[:, :], rowsum_e[:, :]).then_inc(recip_made_e, 1)
                dve.wait_ge(recip_made_e, ph.i)
                for m in range(CH):
                    dve.tensor_scalar(e_sb[:, m, :], e_sb[:, m, :], recip_e[:, m:m + 1], gains[:, 1:2],
                                      ALU.mult, ALU.mult).then_inc(e_made, 1)

            def finish_x1(ph, c, m):
                dve.wait_ge(x_copied, ph.i * (CH * 16) + CH * 16)
                dve.wait_ge(sum_full[m], ph.uses(SUM, f"O0.{c}", m) + 1)
                part = x1[:, m, c * QC:(c + 1) * QC]
                dve.scalar_tensor_tensor(part, sum_ps[m][:, :], vecs[:, C_BIAS, m:m + 1], part,
                                         ALU.add, ALU.add).then_inc(sum_done[m], 1)

            def finish_out(ph, c, m):
                dve.wait_ge(base_made, (ph.i - 1) * CH + (m + 1))
                dve.wait_ge(sum_full[m], ph.uses(SUM, f"O2.{c}", m) + 1)
                part = out_sb[:, m, c * QC:(c + 1) * QC]
                dve.tensor_tensor(part, sum_ps[m][:, :], part, ALU.add).then_inc(sum_done[m], 1)

            def step(ph, name, *numbers):
                n = [int(x) for x in numbers]
                if name == "lG":
                    low_g(ph, f"G.{n[0]}")
                elif name == "lNG":
                    low_g(ph, "NG")
                elif name == "lNV":
                    low_score(ph, "NV", v_l[:, 0:4, :], v_h[:, 0:4, :])
                elif name == "lW":
                    rest()
                elif name in ("lV", "lXT", "lFD"):
                    dst_h, dst_l = {"lV": (v_h, v_l), "lXT": (xt_h, xt_l), "lFD": (fd_h, fd_l)}[name]
                    low_score(ph, f"{name[1:]}.{n[0]}", dst_l[:, 4 * n[0]:4 * n[0] + 4, :],
                              dst_h[:, 4 * n[0]:4 * n[0] + 4, :])
                elif name in ("max0", "max2"):
                    negmax = negmax0 if name == "max0" else negmax2
                    row_max(ph, f"S{name[3]}.{n[0]}", negmax[:, n[0]:n[0] + 1])
                elif name in ("norm0", "norm2"):
                    normalise(ph, name[4], *n)
                elif name in ("lT0", "lT2"):
                    low_turn(ph, name[2], *n)
                elif name == "lFBC":
                    low_fbc(ph)
                elif name == "sA":
                    begin_att(ph)
                elif name == "aA":
                    finish_att(ph)
                elif name == "minE":
                    min_e(ph)
                elif name == "nE":
                    normalise_e(ph)
                elif name == "lET":
                    s = ph.slot(TURN, "ET")
                    dve.wait_ge(turn_staged[s], ph.staged(TURN, "ET") + 1)
                    low(et_l[:, :, :], turn_ps[s][:, :].rearrange("p (m c) -> p m c", c=C), et_h[:, :, :])\
                        .then_inc(turn_done[s], 1)
                elif name == "fx":
                    finish_x1(ph, *n)
                elif name == "fo":
                    finish_out(ph, *n)
                elif name == "bn":
                    bn_stats(ph.i + 1)
                elif name == "spread":
                    spread(ph, ph.i + 1)
                elif name == "gvar":
                    group_var(ph, ph.i + 1)
                elif name == "xn":
                    dve.wait_ge(turn_full[ph.slot(TURN, "T0.7.1")], ph.uses(TURN, "T0.7.1") + 1)
                    make_xn(ph.i + 1, *n)
            phases(dve, DVE_PHASES, step)

        @block.tensor
        def _(pe):
            def product(dst, lhs, rhs, start, stop):
                pe.matmul(dst, lhs[0], rhs[0], start=start, stop=False)
                pe.matmul(dst, lhs[0], rhs[1], start=False, stop=False)
                return pe.matmul(dst, lhs[1], rhs[0], start=False, stop=stop)

            pe.wait_ge(consts_made, 6)

            def group_average(s, n, src, ready, count):
                pe.wait_ge(ready, count)
                if not (isinstance(n, int) and n == 0):
                    pe.wait_ge(turn_done[s], n)
                pe.matmul(turn_ps[s][:, 0:CH * RUNS], group_mean[:, :], src, start=True, stop=True)\
                    .then_inc(turn_full[s], 1)

            def weight_product(ps, lhs, rhs):
                for m in range(CH):
                    for oh in range(CH):
                        last = pe.matmul(ps[:, m * C:(m + 1) * C], lhs[:, oh, m * P:(m + 1) * P], rhs[:, oh, :],
                                         start=(oh == 0), stop=(oh == CH - 1))
                return last

            def bias_product(ps, *terms):
                for m in range(CH):
                    for n, (w, v) in enumerate(terms):
                        for oh in range(CH):
                            last = pe.matmul(ps[:, m:m + 1], w[:, oh, m * P:(m + 1) * P], vecs[:, v, oh:oh + 1],
                                             start=(n == 0 and oh == 0), stop=(n == len(terms) - 1 and oh == CH - 1))
                return last

            def turn_weight(ps, w):
                for m in range(CH):
                    for oh in range(CH):
                        last = pe.transpose(ps[:, m * C + oh * P:m * C + (oh + 1) * P],
                                            w[:, oh, m * P:(m + 1) * P], ident[:, :])
                return last

            group_average(0, 0, bn_parts[:, :, 1], bn_made, CH)
            pe.wait_ge(wo_loaded, 16)
            turn_weight(sum_ps[0], wo_sb).then_inc(wot_turned, 1)
            group_average(1, 0, spread_sb[:, :], turn_done[0], 1)
            pe.wait_ge(wq_loaded, 16)
            pe.wait_ge(wkg_made, 1)
            weight_product(a_ps, wq_sb, wkg_sb).then_inc(a_full, 1)
            pe.wait_ge(wv_loaded, 16)
            pe.wait_ge(wot_made, 1)
            weight_product(b_ps, wv_sb, wot_sb).then_inc(b_full, 1)

            def g_bias():
                pe.wait_ge(g_vecs_loaded, 16 * 2)
                pe.wait_ge(a_copied, 1)
                bias_product(turn_ps[0], (a1_sb, GN_B), (wkg_sb, BQ)).then_inc(g_bias_full, 1)

            def rest():
                pe.wait_ge(block1_loaded, 16 * 3)
                pe.wait_ge(b_copied, 1)
                turn_weight(sum_ps[0], wd_sb)
                for ih in range(CH):
                    for n, w in enumerate((wb_sb, wb_sb, wc_sb)):
                        at = (ih * 3 + n) * C8
                        pe.transpose(sum_ps[1][:, at:at + C8], w[:, ih * P:(ih + 1) * P], ident[0:C8, 0:C8])
                pe.wait_ge(vecs_loaded, 16 * 8)
                bias_product(sum_ps[1][:, C_BIAS_AT:C_BIAS_AT + CH], (b1_sb, GN_B), (wot_sb, BV)).then_inc(rest_full, 1)

            def after(ph, *uses):
                for use in ph.last_uses(SCORE, uses):
                    pe.wait_ge(score_done[ph.slot(SCORE, use)], ph.uses(SCORE, use) + 1)

            def enter(ph, use, *reads):
                s = ph.slot(SCORE, use)
                after(ph, *(r for r in ph.last_uses(SCORE, reads) if ph.slot(SCORE, r) != s))
                wait(pe, score_done[s], ph.uses(SCORE, use))
                return s, score_ps[s]

            def cols(t, n=P):
                return slice(t * n, (t + 1) * n)

            def both(parts, *index):
                return [p[index] for p in parts]

            xn_p, g_p, v_p, x1_p, fd_p = (xn_h, xn_l), (g_h, g_l), (v_h, v_l), (x1_h, x1_l), (fd_h, fd_l)
            pt0_p, pt2_p, xt_p, et_p = (pt0_h, pt0_l), (pt2_h, pt2_l), (xt_h, xt_l), (et_h, et_l)
            every = slice(None)

            def project_g(ph, use, c, ready, count):
                pe.wait_ge(ready, count)
                if use == "G.0":
                    pe.wait_ge(a_made, 1)
                s, ps = enter(ph, use)
                for m in range(CH):
                    if use == "G.0" and m == 1:
                        pe.wait_ge(a_copied, 1)
                    for k in range(CH):
                        last = product(ps[:, cols(m, QC)], both(a_w, every, k, cols(m)),
                                       both(xn_p, every, k, cols(c, QC)), k == 0, k == CH - 1)
                last.then_inc(score_full[s], 1)

            def project_rows(ph, use, u, data, w):
                s, ps = enter(ph, use)
                for t in range(4):
                    for k in range(CH):
                        last = product(ps[:, cols(t, C)], both(data, every, k, cols(4 * u + t)),
                                       both(w, every, k, every), k == 0, k == CH - 1)
                last.then_inc(score_full[s], 1)

            def scores0(ph, j):
                if ph.like == 0 and j == 0:
                    pe.wait_ge(xn_split, XN)
                s, ps = enter(ph, f"S0.{j}", *(["G.0"] if j == 0 and ph.like == 0 else ["G.1"] if j == QT else []))
                for n in range(2):
                    for k in range(CH):
                        last = product(ps[:, cols(n, QC)], both(g_p, every, k, cols(j % QT)),
                                       both(xn_p, every, k, cols(n, QC)), k == 0, k == CH - 1)
                last.then_inc(score_full[s], 1)

            def scores2(ph, j):
                s, ps = enter(ph, f"S2.{j}", *(["FBC"] if j == 0 else []))
                for n in range(2):
                    last = pe.matmul(ps[:, cols(n, QC)], fb_parts[:, cols(j)], fc_parts[:, cols(n, QC)],
                                     start=True, stop=True)
                last.then_inc(score_full[s], 1)

            def enter_turn(ph, use):
                s = ph.slot(TURN, use)
                wait(pe, turn_done[s], ph.uses(TURN, use))
                return s, turn_ps[s]

            def turn(ph, block, j, h):
                made, before = (probs0_made, ph.i) if block == "0" else (probs2_made, ph.i - 1)
                pe.wait_ge(made, before * TILES + (j + 1))
                s, ps = enter_turn(ph, f"T{block}.{j}.{h}")
                rows = probs_of(ph, block, j)
                for t in range(4):
                    last = pe.transpose(ps[:, cols(t)], rows[:, cols(4 * h + t)], ident[:, :])
                last.then_inc(turn_full[s], 1)

            def turn_x1(ph, u):
                if ph.like == 1:
                    for m in range(CH):
                        pe.wait_ge(sum_done[m], CHUNKS)
                s, ps = enter(ph, f"XT.{u}")
                for t in range(4):
                    for k in range(CH):
                        last = pe.transpose(ps[:, t * C + k * P:t * C + (k + 1) * P], x1[:, k, cols(4 * u + t)],
                                            ident[:, :])
                last.then_inc(score_full[s], 1)

            def project_fbc(ph):
                pe.wait_ge(x1_split, ph.i * CH)
                s, ps = enter(ph, "FBC")
                for n in range(2):
                    for k in range(CH):
                        last = product(ps[0:3 * C8, cols(n, QC)], both(bbc_w, every, k, every),
                                       both(x1_p, every, k, cols(n, QC)), k == 0, k == CH - 1)
                last.then_inc(score_full[s], 1)

            def channel_scores(ph):
                s, ps = enter(ph, "ATT", "XT.0", "XT.1")
                for n in range(2):
                    for m in range(CH):
                        for t in range(NT):
                            last = pe.matmul(ps[:, n * QC + m * C:n * QC + (m + 1) * C], xt_h[:, t, cols(m)],
                                             xt_p[n][:, t, :], start=(t == 0), stop=(t == NT - 1))
                last.then_inc(score_full[s], 1)

            def cross_turn(ph):
                a = ph.slot(SCORE, "ATT")
                pe.wait_ge(score_staged[a], ph.staged(SCORE, "ATT") + 1)
                s, ps = enter_turn(ph, "AT")
                for dh in range(CH):
                    for m in range(CH):
                        last = pe.transpose(ps[:, dh * C + m * P:dh * C + (m + 1) * P], cross_sb[:, m, cols(dh)],
                                            ident[:, :])
                last.then_inc(turn_full[s], 1)

            def channel_turn(ph):
                pe.wait_ge(e_made, ph.i * CH)
                s, ps = enter_turn(ph, "ET")
                for dh in range(CH):
                    for m in range(CH):
                        last = pe.transpose(ps[:, dh * C + m * P:dh * C + (m + 1) * P], e_sb[:, m, cols(dh)],
                                            ident[:, :])
                last.then_inc(turn_full[s], 1)

            def turned(ph, uses):
                for use in ph.last_uses(TURN, uses):
                    pe.wait_ge(turn_done[ph.slot(TURN, use)], ph.uses(TURN, use) + 1)

            def sum_steps(ph, block, c):
                v = v_p if block == "0" else fd_p
                pt = turned_of(ph, block, c)
                use = f"O{block}.{c}"
                if block == "2":
                    if c == 0:
                        turned(ph, ["ET"])
                    for m in range(CH):
                        wait(pe, sum_done[m], ph.uses(SUM, use, m))
                        for k in range(CH):
                            last = product(sum_ps[m][:, :], both(et_p, every, k, cols(m)),
                                           both(x1_p, every, k, cols(c, QC)), k == 0, False)
                        if c == CHUNKS - 1 and m == CH - 1:
                            last.then_inc(x1_read, 1)
                        yield
                turned(ph, [f"T{block}.{QT * c + j}.{h}" for j in range(QT) for h in range(2)])
                if c == 0:
                    after(ph, *(["FD.0", "FD.1"] if block == "2" else ["V.0", "V.1"] if ph.like == 0 else ["V.1"]))
                for half, m in ((half, m) for half in range(2) for m in range(CH)):
                    if block == "0" and half == 0:
                        wait(pe, sum_done[m], ph.uses(SUM, use, m))
                        if ph.like == 0 and c == 0:
                            pe.wait_ge(rest_made, 1)
                    for k in range(half * NT // 2, (half + 1) * NT // 2):
                        last = product(sum_ps[m][:, :], both(v, every, k, cols(m)), both(pt, every, k, every),
                                       block == "0" and k == 0, k == NT - 1)
                        if k == NT - 1:
                            last.then_inc(sum_full[m], 1)
                        yield

            sums = {}

            def sum_on(ph, block, c, steps):
                key = ph.like, block, c
                if key not in sums:
                    sums[key] = sum_steps(ph, block, c)
                for _ in range(steps):
                    next(sums[key])

            def stats(ph, use):
                s = ph.slot(TURN, use)
                if use == "MEAN":
                    group_average(s, ph.uses(TURN, use), bn_parts[:, :, 1], bn_made, ph.i * CH + 2 * CH)
                else:
                    m = ph.slot(TURN, "MEAN")
                    group_average(s, 0 if m == s else ph.uses(TURN, use), spread_sb[:, :], turn_done[m],
                                  ph.uses(TURN, use) if m == s else ph.uses(TURN, "MEAN") + 1)

            def step(ph, name, *numbers):
                if name in ("O0", "O2"):
                    sum_on(ph, name[1], int(numbers[0]), int(numbers[1][1:]))
                    return
                n = [int(x) for x in numbers]
                if name == "G":
                    project_g(ph, f"G.{n[0]}", n[0], *((x0_low, 1) if ph.like == 0 and n[0] == 0 else
                                                       (xn_split, ph.i * XN + XN)))
                elif name == "NG":
                    project_g(ph, "NG", 0, xn_split, ph.i * XN + 2 * XN)
                elif name == "NV":
                    pe.wait_ge(xn_split, ph.i * XN + 2 * XN)
                    project_rows(ph, "NV", 0, xn_p, b_w)
                elif name == "BG":
                    g_bias()
                elif name == "W":
                    rest()
                elif name == "V":
                    if ph.like == 0 and n[0] == 0:
                        pe.wait_ge(b_made, 1)
                        pe.wait_ge(b_copied, 1)
                    else:
                        pe.wait_ge(xn_split, ph.i * XN + XN)
                    project_rows(ph, f"V.{n[0]}", n[0], xn_p, b_w)
                elif name == "FD":
                    pe.wait_ge(x1_split, ph.i * CH)
                    project_rows(ph, f"FD.{n[0]}", n[0], x1_p, d_w)
                elif name == "S0":
                    scores0(ph, *n)
                elif name == "S2":
                    scores2(ph, *n)
                elif name in ("T0", "T2"):
                    turn(ph, name[1], *n)
                elif name == "XT":
                    turn_x1(ph, *n)
                elif name == "FBC":
                    project_fbc(ph)
                elif name == "ATT":
                    channel_scores(ph)
                elif name == "AT":
                    cross_turn(ph)
                elif name == "ET":
                    channel_turn(ph)
                elif name in STATS:
                    stats(ph, name)
            phases(pe, PE_PHASES, step)


_INS = ["x"] + [f"L0_conv_{n}" for n in ("gn_w", "gn_b", "wq", "bq", "wk", "bk", "wv", "bv", "wo", "bo")] \
    + [f"L1_conv_{n}" for n in ("wb", "bb", "wc", "bc", "wd", "bd", "alpha", "beta")]
_OUTS = [((BATCH, C, 32, 32), "float32")]


def kernel(**inputs):
    import numpy as _np
    import concourse.bacc as _bacc
    from concourse import mybir as _mybir
    from concourse.bass_utils import run_bass_kernel_spmd as _run

    nc = _bacc.Bacc("TRN2", target_bir_lowering=False, num_devices=1)
    arrays, args = {}, []
    for name in _INS:
        a = _np.ascontiguousarray(inputs[name])
        arrays[f"in_{name}_dram"] = a
        args.append(nc.dram_tensor(f"in_{name}_dram", a.shape, _mybir.dt.from_np(a.dtype), kind="ExternalInput").ap())
    for i, (shape, dtype) in enumerate(_OUTS):
        dt = _mybir.dt.from_np(_np.dtype(dtype))
        args.append(nc.dram_tensor(f"out_{i}_dram", shape, dt, kind="ExternalOutput").ap())
    dual_attention_kernel(nc, *args)
    r = _run(nc, [arrays], core_ids=[0])
    return r.results[0]["out_0_dram"]
```
